# Optimizing a Trainium2 kernel written in Bass

```python
import numpy as np
import jax
import jax.numpy as jnp

def _softmax(x, axis=-1):
    return jax.nn.softmax(x, axis=axis)

def _gelu(x):
    return jax.nn.gelu(x, approximate=True)

def _silu(x):
    return jax.nn.silu(x)

def _sigmoid(x):
    return jax.nn.sigmoid(x)

def _layernorm(x, axis=-1, eps=1e-05):
    m = jnp.mean(x, axis=axis, keepdims=True)
    v = jnp.var(x, axis=axis, keepdims=True)
    return (x - m) / jnp.sqrt(v + eps)

def _scatter_add(tgt, idx, src, axis=0):
    return tgt.at[idx].add(src)

def _segment_sum(src, seg, n):
    return jax.ops.segment_sum(src, seg, n)
kernel_name = 'mk_xattn_ffn_d1_seqx_r8_eff607'

def setup_inputs(seed: int=0):
    np.random.seed(seed)
    _w = jnp.asarray

    def _rec_inputs():
        import jax
        import jax.numpy as jnp
        _rk = jax.random.key(seed)
        x = -0.0002928 + 1 * jax.random.normal(jax.random.fold_in(_rk, 1), (64, 64, 128), jnp.float32)
        _lenS = 64 - jax.random.randint(jax.random.fold_in(_rk, 7), (64,), 0, max(1, 64 // 4) + 1, jnp.int32)
        _lenS2 = 64 - jax.random.randint(jax.random.fold_in(_rk, 8), (64,), 0, max(1, 64 // 4) + 1, jnp.int32)
        _ctx_1024P = jax.random.normal(jax.random.fold_in(_rk, 11), (64, 16, 128), jnp.float32)
        _ctx_1024c = jax.random.dirichlet(jax.random.fold_in(_rk, 511), 0.3 * jnp.ones((16,), jnp.float32), (64, 64))
        _ctx_1024t = jnp.einsum('bsk,bkd->bsd', _ctx_1024c, _ctx_1024P)
        _ctx_1024t = _ctx_1024t * jax.lax.rsqrt(jnp.mean(jnp.square(_ctx_1024t)) + 1e-12) * 0.953939
        ctx_1024 = -1.39393e-06 + 0.999914 * (_ctx_1024t + 0.3 * jax.random.normal(jax.random.fold_in(_rk, 611), (64, 64, 128), jnp.float32))
        return (x, ctx_1024)
    x, ctx_1024 = _rec_inputs()

    def _L0_xattn_setup():
        import jax, jax.numpy as jnp
        import numpy as np
        B, S, D = (1, 512, 128)
        NUM_HEADS, HEAD_DIM = (16, 64)
        WINDOW = 128
        EMBED = NUM_HEADS * HEAD_DIM
        key = jax.random.key(seed)
        ks = jax.random.split(key, 7)
        scale_in = 1.0 / np.sqrt(D)
        scale_e = 1.0 / np.sqrt(EMBED)
        return {'query': jax.random.normal(ks[0], (B, S, D), dtype=jnp.float32), 'key': jax.random.normal(ks[1], (B, S, D), dtype=jnp.float32), 'value': jax.random.normal(ks[2], (B, S, D), dtype=jnp.float32), 'Wq': jax.random.normal(ks[3], (D, EMBED), dtype=jnp.float32) * scale_in, 'Wk': jax.random.normal(ks[4], (D, EMBED), dtype=jnp.float32) * scale_in, 'Wv': jax.random.normal(ks[5], (D, EMBED), dtype=jnp.float32) * scale_in, 'Wo': jax.random.normal(ks[6], (EMBED, D), dtype=jnp.float32) * scale_e}
    _L0_xattn_all = _L0_xattn_setup()
    _L0_xattn_in = {k: v for k, v in _L0_xattn_all.items() if k in ('Wq', 'Wk', 'Wv', 'Wo')}
    del _L0_xattn_all

    def _L0_ffn_setup():
        import jax, jax.numpy as jnp
        import numpy as np
        EPS = 1e-06
        N_EXPERTS = 8

        def _rms_norm(x, scale, eps=EPS):
            mean_sq = jnp.mean(x.astype(jnp.float32) ** 2, axis=-1, keepdims=True)
            s = scale.astype(jnp.float32) * jax.lax.rsqrt(mean_sq + eps)
            return x * s.astype(x.dtype)

        def _dist2(x, y):
            nx = jnp.sum(x ** 2, axis=-1)[..., :, None]
            ny = jnp.sum(y ** 2, axis=-1)[..., None, :]
            return nx + ny - 2.0 * (x @ y.T)
        key = jax.random.key(seed)
        ks = jax.random.split(key, 5)
        dim, hidden, E = (128, 256, N_EXPERTS)
        x = jax.random.normal(ks[0], (4, 256, dim), dtype=jnp.float32)
        scale = jnp.ones((dim,), dtype=jnp.float32)
        centroids = jax.random.normal(ks[1], (E, dim), dtype=jnp.float32)
        up_w = jax.random.normal(ks[2], (E, dim, hidden * 2), dtype=jnp.float32) * dim ** (-0.5)
        down_w = jax.random.normal(ks[3], (E, hidden, dim), dtype=jnp.float32) * hidden ** (-0.5)
        return {'x': x, 'scale': scale, 'centroids': centroids, 'up_w': up_w, 'down_w': down_w}
    _L0_ffn_all = _L0_ffn_setup()
    _L0_ffn_in = {k: v for k, v in _L0_ffn_all.items() if k in ('scale', 'centroids', 'up_w', 'down_w')}
    del _L0_ffn_all
    return {'x': x, 'ctx_1024': ctx_1024, 'L0_xattn_Wq': _L0_xattn_in['Wq'], 'L0_xattn_Wk': _L0_xattn_in['Wk'], 'L0_xattn_Wv': _L0_xattn_in['Wv'], 'L0_xattn_Wo': _L0_xattn_in['Wo'], 'L0_ffn_scale': _L0_ffn_in['scale'], 'L0_ffn_centroids': _L0_ffn_in['centroids'], 'L0_ffn_up_w': _L0_ffn_in['up_w'], 'L0_ffn_down_w': _L0_ffn_in['down_w']}

def reference(x, ctx_1024, L0_xattn_Wq, L0_xattn_Wk, L0_xattn_Wv, L0_xattn_Wo, L0_ffn_scale, L0_ffn_centroids, L0_ffn_up_w, L0_ffn_down_w):
    import jax
    import jax.numpy as jnp

    def _L0_xattn_ref(query, key, value, Wq, Wk, Wv, Wo):
        import jax, jax.numpy as jnp
        import numpy as np
        B, S, D = (1, 512, 128)
        NUM_HEADS, HEAD_DIM = (16, 64)
        WINDOW = 128
        EMBED = NUM_HEADS * HEAD_DIM
        Bq, Sq, _ = query.shape
        q = (query @ Wq).reshape(Bq, Sq, NUM_HEADS, HEAD_DIM).transpose(0, 2, 1, 3)
        k = (key @ Wk).reshape(Bq, Sq, NUM_HEADS, HEAD_DIM).transpose(0, 2, 1, 3)
        v = (value @ Wv).reshape(Bq, Sq, NUM_HEADS, HEAD_DIM).transpose(0, 2, 1, 3)
        idx = jnp.arange(Sq)
        local_mask = jnp.abs(idx[:, None] - idx[None, :]) > WINDOW
        scores = jnp.einsum('bhqd,bhkd->bhqk', q, k) / jnp.sqrt(jnp.float32(HEAD_DIM))
        scores = jnp.where(local_mask, -jnp.inf, scores)
        attn = jax.nn.softmax(scores, axis=-1)
        out = jnp.einsum('bhqk,bhkd->bhqd', attn, v)
        out = out.transpose(0, 2, 1, 3).reshape(Bq, Sq, EMBED)
        return out @ Wo

    def _L0_ffn_ref(x, scale, centroids, up_w, down_w):
        import jax, jax.numpy as jnp
        import numpy as np
        EPS = 1e-06
        N_EXPERTS = 8

        def _rms_norm(x, scale, eps=EPS):
            mean_sq = jnp.mean(x.astype(jnp.float32) ** 2, axis=-1, keepdims=True)
            s = scale.astype(jnp.float32) * jax.lax.rsqrt(mean_sq + eps)
            return x * s.astype(x.dtype)

        def _dist2(x, y):
            nx = jnp.sum(x ** 2, axis=-1)[..., :, None]
            ny = jnp.sum(y ** 2, axis=-1)[..., None, :]
            return nx + ny - 2.0 * (x @ y.T)
        skip = x
        xn = _rms_norm(x, scale)
        ids = jnp.argmin(_dist2(xn, centroids), axis=-1)
        out = jnp.zeros_like(x)
        for e in range(N_EXPERTS):
            h = jnp.einsum('bsd,dh->bsh', xn, up_w[e])
            a, g = jnp.split(h, 2, axis=-1)
            y = jnp.einsum('bsh,hd->bsd', a * jax.nn.silu(g), down_w[e])
            out = jnp.where((ids == e)[..., None], y, out)
        return out + skip
    x = x + _L0_xattn_ref(_layernorm(x, axis=-1), ctx_1024, ctx_1024, L0_xattn_Wq, L0_xattn_Wk, L0_xattn_Wv, L0_xattn_Wo)
    x = x + _L0_ffn_ref(_layernorm(x, axis=-1), L0_ffn_scale, L0_ffn_centroids, L0_ffn_up_w, L0_ffn_down_w)
    return x

_drawn_inputs = setup_inputs


def setup_inputs(seed=0):
    import zlib

    import numpy as np

    out = dict(_drawn_inputs(seed))
    spreads = {'L0_ffn_scale': (1.0, 0.2)}
    factors = {}
    for name, (base, spread) in spreads.items():
        noise = np.random.default_rng([zlib.crc32(name.encode()), seed]).standard_normal(out[name].shape)
        drawn = base * np.exp(spread * noise) if base else spread * noise
        out[name] = jnp.asarray(drawn.astype(out[name].dtype))
    for name, factor in factors.items():
        out[name] = (out[name] * factor).astype(out[name].dtype)
    return out
```

```python
from contextlib import ExitStack

import concourse.bass as bass
from concourse import mybir

F32 = mybir.dt.float32
F32R = mybir.dt.float32r
BF16 = mybir.dt.bfloat16
U32 = mybir.dt.uint32
I32 = mybir.dt.int32
ALU = mybir.AluOpType
ACT = mybir.ActivationFunctionType
AX_X = mybir.AxisListType.X

P = 128
D = 128
SEQ = 64
TOKENS = 4096
HEADS = 16
HD = 64
TILES = TOKENS // P
TPG = 4
GROUPS = TILES // TPG
GT = TPG * P
HALF = HEADS // 2 * SEQ
BLK = 32
NBLK = HEADS * SEQ // BLK
SCORE_SCALE = HD ** -0.5
LN_EPS = 1e-5
RMS_EPS = 1e-6

EXPERTS = 8
HID = 256
ROW = 2 * D + 4
ID_AT = 2 * D
REGION = TOKENS + P
NO_TOKEN = 1 << 20
FT = 40
FB = 4
HEADS_AT = {0: ([], []), 1: ([0, 1, 2], [3, 4, 5]), 2: ([6, 7, 8], [9, 10, 11]), 3: ([12], [13, 14, 15])}
LOOPS = (GROUPS - 2) // 2


def xattn_ffn(nc, x, ctx, ctx_t, wq_t, wk_t, wv_t, wo, scale, cent_t, up_w, down_w, out):
    x_v = x.rearrange("(g t p) d -> g p t d", t=TPG, p=P)
    ctx_v = ctx.rearrange("(g t p) d -> g p t d", t=TPG, p=P)
    ctxt_v = ctx_t.rearrange("d (g n) -> g d n", g=GROUPS)
    table = nc.dram_tensor("sorted_rows", (EXPERTS * REGION + FT * P, ROW), F32)

    with ExitStack() as es:
        def sb(name, shape, dt=F32):
            return es.enter_context(nc.sbuf_tensor(name, shape, dt))

        def sem(name):
            return es.enter_context(nc.semaphore(name))

        banks = [es.enter_context(nc.psum_tensor(f"bank{i}", [P, 512], F32)) for i in range(8)]
        S_BANK = [banks[0:2], banks[2:4]]
        G_BANK = banks[4:6]
        Y_BANK, MISC = banks[4], banks[5]
        U_BANK = banks[6:8]

        a_hi = sb("a_hi", [P, HEADS, D], F32R)
        a_lo = sb("a_lo", [P, HEADS, D], F32R)
        m_sb = sb("m_sb", [P, HEADS, D])
        upw = sb("upw", [P, EXPERTS * 2 * HID])
        downw = sb("downw", [P, EXPERTS * 2 * D])
        scale_b = sb("scale_b", [P, D])
        centT = sb("centT", [P, EXPERTS])
        cent_sq = sb("cent_sq", [P, EXPERTS])
        cent_norm = sb("cent_norm", [P, EXPERTS])
        ident = sb("ident", [P, P])
        id32f = sb("id32f", [P, BLK])
        id32b = sb("id32b", [P, BLK], BF16)
        blk_f = sb("blk_f", [P, P])
        blk_b = sb("blk_b", [P, P], BF16)
        blk_r = sb("blk_r", [P, P], F32R)
        ones_f = sb("ones_f", [P, P])
        ones_b = sb("ones_b", [P, P], BF16)
        before_b = sb("before_b", [P, P], BF16)
        expert_m8 = sb("expert_m8", [P, EXPERTS])
        region_of = sb("region_of", [P, EXPERTS])

        xin = sb("xin", [P, TPG, D])
        xres = sb("xres", [P, 2, TPG, D])
        ctxT = sb("ctxT", [P, 2, GT])
        ctxN = sb("ctxN", [P, 2, TPG, D])
        stats1 = sb("stats1", [P, TPG, 6])
        mv1 = sb("mv1", [P, TPG, 2])
        var1 = sb("var1", [P, TPG])
        rstd1 = sb("rstd1", [P, TPG])
        xln = sb("xln", [P, TPG, D])
        xT_hi = sb("xT_hi", [P, GT], F32R)
        xT_lo = sb("xT_lo", [P, GT], F32R)
        gq = sb("gq", [P, 2, HEADS, GT])
        turned = sb("turned", [P, 2 * HALF])
        turned_p = sb("turned_p", [P, 2 * HALF])
        key_max = sb("key_max", [P, NBLK])
        key_max2 = sb("key_max2", [P, NBLK])
        top = sb("top", [P, NBLK])
        neg_max = sb("neg_max", [P, 2, NBLK], BF16)
        max_rows = sb("max_rows", [P, 2, 2 * HALF], BF16)
        probs = sb("probs", [P, 2, 2 * HALF])
        key_sum = sb("key_sum", [P, NBLK])
        key_sum2 = sb("key_sum2", [P, NBLK])
        total = sb("total", [P, NBLK])
        inv = sb("inv", [P, 2, NBLK])
        inv_hi = sb("inv_hi", [P, NBLK], F32R)
        inv_rows = sb("inv_rows", [P, 2, 2 * HALF], F32R)
        ut = sb("ut", [P, 2, HEADS, P])
        weights = ut[:].rearrange("p a (b h) d -> p (a b) h d", b=2)
        wqT, wkT, wvT, wo_sb = (weights[:, n] for n in range(4))
        x2 = sb("x2", [P, TPG, D])
        stats2 = sb("stats2", [P, TPG, 6])
        mv2 = sb("mv2", [P, TPG, 2])
        spread2 = sb("spread2", [P, 2, TPG])
        var_inv = sb("var_inv", [P, TPG])
        root2 = sb("root2", [P, 2, TPG])
        power = sb("power", [P, 2 * TPG])
        xl = sb("xl", [P, TPG, D])
        square = sb("square", [P, TPG, D])
        norm2 = sb("norm2", [P, TPG])
        rows = sb("rows", [P, 2, TPG, ROW])
        xnT = sb("xnT", [P, GT])
        norms = sb("norms", [P, TPG, EXPERTS])
        dist = sb("dist", [P, TPG, EXPERTS])
        least = sb("least", [P, TPG])
        cand = sb("cand", [P, TPG, EXPERTS])
        chosen = sb("chosen", [P, TPG])
        onehot = sb("onehot", [P, TPG, EXPERTS], BF16)
        earlier = sb("earlier", [P, TPG, EXPERTS], BF16)
        seen = sb("seen", [P, EXPERTS], BF16)
        place = sb("place", [P, TPG, EXPERTS])
        place_f = sb("place_f", [P, TPG])
        place_u = sb("place_u", [P, 2, TPG], U32)
        token_f = sb("token_f", [P, TPG])

        count = sb("count", [P, EXPERTS])
        count_i = sb("count_i", [P, EXPERTS], I32)
        ntile = sb("ntile", [P, EXPERTS])
        upto = sb("upto", [P, EXPERTS, EXPERTS])
        cumul = sb("cumul", [P, EXPERTS])
        pad_at = sb("pad_at", [P, EXPERTS])
        pad_u = sb("pad_u", [P, EXPERTS], U32)
        part_f = sb("part_f", [P, 1])
        pad_row = sb("pad_row", [P, ROW])
        tile_no = sb("tile_no", [P, FT])
        done = sb("done", [P, FT, EXPERTS])
        done_n = sb("done_n", [P, FT, EXPERTS])
        tile_e = sb("tile_e", [P, FT])
        tile_b = sb("tile_b", [P, FT])
        tile_r = sb("tile_r", [P, FT])
        t_expert = sb("t_expert", [P, FT], I32)
        t_row = sb("t_row", [P, FT], I32)

        spare_v = sb("spare_v", [P, 1])
        spare_p = sb("spare_p", [P, 3])
        room = gq[:, 0].rearrange("p h n -> p (h n)")
        taken = [0]

        def from_queries(shape):
            n = shape[0] * shape[1]
            taken[0] += n
            return room[:, taken[0] - n:taken[0]].rearrange("p (a b) -> p a b", a=shape[0])

        frow = from_queries([FB, ROW])
        fxT = from_queries([2, P])
        gate = from_queries([2, HID])
        act = from_queries([2, HID])
        actT = from_queries([2, HID])
        fout = from_queries([FB, D])

        weights_in = sem("weights_in")
        ffn_in = sem("ffn_in")
        small_in = sem("small_in")
        x_in = sem("x_in")
        xres_in = sem("xres_in")
        ctxT_in = sem("ctxT_in")
        ctxN_in = sem("ctxN_in")
        pool_seq = sem("pool_seq")
        consts_made = sem("consts_made")
        dve_seq = sem("dve_seq")
        consts_cast = sem("consts_cast")
        fold_ready = sem("fold_ready")
        a_rest = sem("a_rest")
        m_copied = sem("m_copied")
        a_split = sem("a_split")
        norm_ready = sem("norm_ready")
        norm_taken = sem("norm_taken")
        var1_done = sem("var1_done")
        rstd1_done = sem("rstd1_done")
        spread2_done = sem("spread2_done")
        root2_done = sem("root2_done")
        ln1_done = sem("ln1_done")
        xT_ready = sem("xT_ready")
        xT_hi_out = sem("xT_hi_out")
        xT_lo_out = sem("xT_lo_out")
        g_ready = sem("g_ready")
        g_out = sem("g_out")
        scores_ready = sem("scores_ready")
        max_found = sem("max_found")
        max_spread = sem("max_spread")
        shifted = sem("shifted")
        exp_done = sem("exp_done")
        inv_found = sem("inv_found")
        inv_spread = sem("inv_spread")
        inv_ready = sem("inv_ready")
        probs_ready = sem("probs_ready")
        u_ready = sem("u_ready")
        u_out = sem("u_out")
        y_ready = sem("y_ready")
        x2_done = sem("x2_done")
        xl_done = sem("xl_done")
        base_done = sem("base_done")
        xn_done = sem("xn_done")
        xnT_ready = sem("xnT_ready")
        xnT_out = sem("xnT_out")
        dots_ready = sem("dots_ready")
        dots_taken = sem("dots_taken")
        onehot_done = sem("onehot_done")
        ranks_ready = sem("ranks_ready")
        ranks_taken = sem("ranks_taken")
        place_done = sem("place_done")
        scattered = sem("scattered")
        counts_ready = sem("counts_ready")
        pads_found = sem("pads_found")
        padded = sem("padded")
        tiles_found = sem("tiles_found")
        frow_in = [sem(f"frow{k}_in") for k in range(FB)]
        fxT_ready = sem("fxT_ready")
        fxT_out = sem("fxT_out")
        up_ready = sem("up_ready")
        gated = sem("gated")
        act_done = sem("act_done")
        actT_ready = sem("actT_ready")
        actT_out = sem("actT_out")
        down_ready = sem("down_ready")
        fout_done = sem("fout_done")
        settled = sem("settled")
        stored = [sem(f"out{k}_stored") for k in range(FB)]

        block = es.enter_context(nc.Block())

        def groups(eng, group, per_group=None):
            group(0, 0, False, True)
            with eng.Fori(0, LOOPS) as i:
                for k in range(2):
                    group(1 + k + 2 * i, (1 + k) % 2, True, True)
            group(GROUPS - 1, (GROUPS - 1) % 2, True, False)

        def ffn_steps(eng, step):
            for k in range(FB):
                step(k, k, 0, k)
            with eng.Fori(1, FT // FB) as i:
                for k in range(FB):
                    step(FB * i + k, k, i, FB + k)
            for k in range(2):
                step(FT + k, k, FT // FB, FT + k)

        def settle_v():
            return nc.vector.memset(spare_v[:], 0.0)

        def settle_p(column):
            return nc.gpsimd.tensor_tensor(spare_p[:, column:column + 1], part_f[:], part_f[:], ALU.add)

        class Chain:

            def __init__(self, eng, sem):
                self.eng, self.sem, self.base, self.n = eng, sem, 0, 0

            def mark(self, ins):
                ins.then_inc(self.sem, 1)
                self.n += 1

            def wait(self):
                self.eng.wait_ge(self.sem, self.base + self.n)

            def then(self, ins):
                self.mark(ins)
                self.wait()

            def loop(self, i, per_turn):
                self.start = self.n
                self.base, self.n = self.n + i * per_turn, 0
                self.per_turn = per_turn

            def end_loop(self, turns):
                assert self.n == self.per_turn, (self.n, self.per_turn)
                self.base, self.n = 0, self.start + turns * self.per_turn

        @block.sync
        def _(sp):
            sp.dma_start(wqT, wq_t.rearrange("(c p) d -> p c d", p=P)).then_inc(weights_in, 16)
            sp.dma_start(wkT, wk_t.rearrange("(c p) d -> p c d", p=P)).then_inc(weights_in, 16)
            sp.dma_start(wvT, wv_t.rearrange("(c p) d -> p c d", p=P)).then_inc(weights_in, 16)
            sp.dma_start(wo_sb, wo.rearrange("(c p) d -> p c d", p=P)).then_inc(weights_in, 16)
            sp.dma_start(xin[:], x_v[0]).then_inc(x_in, 16)
            sp.dma_start(ctxT[:, 0, :], ctxt_v[0]).then_inc(ctxT_in, 16)
            sp.dma_start(ctxN[:, 0], ctx_v[0]).then_inc(ctxN_in, 16)
            sp.dma_start(xres[:, 0], x_v[0]).then_inc(xres_in, 16)
            sp.dma_start(scale_b[:], scale.to_broadcast([P, D])).then_inc(small_in, 16)
            sp.dma_start(centT[:], cent_t).then_inc(small_in, 16)
            sp.dma_start(upw[:].rearrange("p (e h) -> p e h", e=EXPERTS),
                         up_w.rearrange("e d h -> d e h")).then_inc(ffn_in, 16)
            sp.dma_start(downw[:].rearrange("p (e c d) -> p e c d", e=EXPERTS, c=2),
                         down_w.rearrange("e (c p) d -> p e c d", p=P)).then_inc(ffn_in, 16)

            def group(g, par, has_prev, has_next):
                if not has_next:
                    return
                sp.wait_ge(ln1_done, TPG * (g + 1))
                sp.dma_start(xin[:], x_v[g + 1]).then_inc(x_in, 16)
                sp.wait_ge(ctxT_in, 16 * (g + 1))
                if has_prev:
                    sp.wait_ge(x2_done, TPG * g)
                sp.dma_start(ctxT[:, 1 - par, :], ctxt_v[g + 1]).then_inc(ctxT_in, 16)
                sp.wait_ge(ctxN_in, 16 * (g + 1))
                sp.dma_start(ctxN[:, 1 - par], ctx_v[g + 1]).then_inc(ctxN_in, 16)
                sp.wait_ge(xres_in, 16 * (g + 1))
                sp.dma_start(xres[:, 1 - par], x_v[g + 1]).then_inc(xres_in, 16)

            groups(sp, group)

            sp.wait_ge(tiles_found, 1)
            sp.wait_ge(padded, 16 * EXPERTS)
            sp.wait_ge(scattered, 16 * (TILES + 1))

            def step(j, k, turn, static):
                if static >= FT:
                    return
                if static >= FB:
                    sp.wait_ge(stored[k], 16 * turn)
                row = sp.value_load(t_row[0:1, bass.ds(j, 1)], min_val=0, max_val=(EXPERTS * REGION + (FT - 1) * P))
                sp.dma_start(frow[:, k, :], table[bass.ds(row, P), :]).then_inc(frow_in[k], 16)

            ffn_steps(sp, step)

        @block.gpsimd
        def _(pool):
            seq = Chain(pool, pool_seq)
            nc.gpsimd.memset(ones_f[:], 1.0).then_inc(pool_seq, 1)
            nc.gpsimd.memset(ident[:], 0.0).then_inc(pool_seq, 1)
            nc.gpsimd.memset(id32f[:], 0.0).then_inc(pool_seq, 1)
            nc.gpsimd.memset(blk_f[:], 0.0).then_inc(pool_seq, 1)
            nc.gpsimd.memset(pad_row[:], 0.0).then_inc(pool_seq, 1)
            nc.gpsimd.memset(rows[:], 0.0).then_inc(pool_seq, 1)
            seq.n = 6
            seq.wait()
            seq.mark(nc.gpsimd.affine_select(out=ident[:], in_=ident[:], compare_op=ALU.not_equal, fill=1.0,
                                             base=0, pattern=[[-1, P]], channel_multiplier=1))
            for q in range(P // BLK):
                seq.then(nc.gpsimd.affine_select(out=id32f[:], in_=id32f[:], compare_op=ALU.not_equal, fill=1.0,
                                                 base=-BLK * q, pattern=[[-1, BLK]], channel_multiplier=1))
            for q in range(P // SEQ):
                seq.then(nc.gpsimd.memset(blk_f[q * SEQ:(q + 1) * SEQ, q * SEQ:(q + 1) * SEQ], 1.0))
            seq.mark(nc.gpsimd.iota(expert_m8[:], pattern=[[1, EXPERTS]], base=-EXPERTS, channel_multiplier=0,
                                    allow_small_or_imprecise_dtypes=True))
            seq.mark(nc.gpsimd.iota(region_of[:], pattern=[[REGION, EXPERTS]], base=0, channel_multiplier=0,
                                    allow_small_or_imprecise_dtypes=True))
            seq.mark(nc.gpsimd.iota(token_f[:], pattern=[[P, TPG]], base=0, channel_multiplier=1,
                                    allow_small_or_imprecise_dtypes=True))
            seq.mark(nc.gpsimd.iota(part_f[:], pattern=[[0, 1]], base=0, channel_multiplier=1,
                                    allow_small_or_imprecise_dtypes=True))
            seq.mark(nc.gpsimd.iota(tile_no[:], pattern=[[1, FT]], base=0, channel_multiplier=0,
                                    allow_small_or_imprecise_dtypes=True))
            seq.mark(nc.gpsimd.iota(pad_row[:, ID_AT:ID_AT + 1].bitcast(I32), pattern=[[0, 1]], base=NO_TOKEN,
                                    channel_multiplier=0))
            seq.mark(nc.gpsimd.memset(upto[:], 1.0))
            seq.mark(nc.gpsimd.memset(before_b[:], 1.0))
            seq.wait()
            seq.mark(nc.gpsimd.affine_select(out=upto[:], in_=upto[:], compare_op=ALU.is_ge, fill=0.0, base=0,
                                             pattern=[[1, EXPERTS], [-1, EXPERTS]], channel_multiplier=0))
            seq.mark(nc.gpsimd.affine_select(out=before_b[:], in_=before_b[:], compare_op=ALU.is_gt, fill=0.0,
                                             base=0, pattern=[[1, P]], channel_multiplier=-1))
            seq.wait()
            nc.gpsimd.memset(power[:], -0.5).then_inc(consts_made, 1)
            nc.gpsimd.memset(seen[:], 0.0).then_inc(consts_made, 1)
            pool.dma_start(table[EXPERTS * REGION:, :].rearrange("(t p) r -> p t r", p=P),
                           pad_row[:].unsqueeze(1).to_broadcast([P, FT, ROW])).then_inc(scattered, 16)
            pool.wait_ge(consts_cast, 4)

            pool.wait_ge(consts_made, 2)

            def root_x(g):
                pool.wait_ge(var1_done, g + 1)
                nc.gpsimd.tensor_tensor(rstd1[:], var1[:], power[:, 0:TPG], ALU.pow).then_inc(rstd1_done, 1)

            def root_x2(g):
                pool.wait_ge(spread2_done, g + 1)
                nc.gpsimd.tensor_tensor(root2[:].rearrange("p a t -> p (a t)"),
                                        spread2[:].rearrange("p a t -> p (a t)"), power[:],
                                        ALU.pow).then_inc(root2_done, 1)

            def spread_max(s, par):
                pool.wait_ge(max_found, 3 * (s + 1))
                if not (isinstance(s, int) and s < 2):
                    pool.wait_ge(shifted, s - 1)
                nc.gpsimd.tensor_tensor(
                    max_rows[:, par].rearrange("p (b j) -> p b j", j=BLK),
                    neg_max[:, par].unsqueeze(2).to_broadcast([P, NBLK, BLK]),
                    id32b[:].unsqueeze(1).to_broadcast([P, NBLK, BLK]), ALU.mult).then_inc(max_spread, 1)

            def spread_inv(s, par):
                pool.wait_ge(inv_found, 2 * (s + 1))
                if not (isinstance(s, int) and s < 2):
                    pool.wait_ge(inv_ready, s - 1)
                nc.gpsimd.tensor_tensor(
                    inv_rows[:, par].rearrange("p (b j) -> p b j", j=BLK),
                    inv[:, par].unsqueeze(2).to_broadcast([P, NBLK, BLK]),
                    id32f[:].unsqueeze(1).to_broadcast([P, NBLK, BLK]), ALU.mult).then_inc(inv_spread, 1)

            def residual(g, par):
                pool.wait_ge(xl_done, TPG * (g + 1))
                nc.gpsimd.tensor_tensor(rows[:, par, :, D:2 * D], x2[:], xl[:], ALU.add).then_inc(base_done, 1)
                nc.gpsimd.tensor_copy(rows[:, par, :, ID_AT:ID_AT + 1].bitcast(U32),
                                      token_f[:].unsqueeze(2)).then_inc(base_done, 1)
                pool.wait_ge(base_done, 3 * g + 2)
                settle_p(0)
                nc.gpsimd.tensor_scalar(token_f[:], token_f[:], float(GT), None, ALU.add).then_inc(base_done, 1)

            def scatter(g, par):
                pool.wait_ge(place_done, g + 1)
                pool.wait_ge(xn_done, TPG * (g + 1))
                pool.wait_ge(base_done, 3 * (g + 1))
                settle_p(1)
                for t in range(TPG):
                    pool.indirect_dma_start(
                        out=table[:, :], out_offset=bass.IndirectOffsetOnAxis(ap=place_u[:, par, t:t + 1], axis=0),
                        in_=rows[:, par, t, :], in_offset=None).then_inc(scattered, 16)

            def group(g, par, has_prev, has_next):
                for t in range(TPG):
                    s = TPG * g + t
                    if t == 0 and has_next:
                        root_x(g + 1)
                    if t == 2 and has_prev:
                        root_x2(g - 1)
                    spread_max(s, t % 2)
                    if t >= 1 or has_prev:
                        spread_inv(s - 1, (t + 1) % 2)
                    if t == 2 and has_prev:
                        residual(g - 1, 1 - par)
                    if t == 3 and has_prev:
                        scatter(g - 1, 1 - par)

            root_x(0)
            groups(pool, group)
            spread_inv(TILES - 1, 1)
            last = GROUPS - 1
            root_x2(last)
            residual(last, last % 2)
            scatter(last, last % 2)

            pool.wait_ge(pads_found, 1)
            for e in range(EXPERTS):
                pool.indirect_dma_start(
                    out=table[:, :], out_offset=bass.IndirectOffsetOnAxis(ap=pad_u[:, e:e + 1], axis=0),
                    in_=pad_row[:], in_offset=None).then_inc(padded, 16)

            def step(j, k, turn, static):
                if static < 2:
                    return
                k = (k - 2) % FB
                pool.wait_ge(fout_done, j - 1)
                pool.wait_ge(settled, j - 2)
                settle_p(2).then_inc(settled, 1)
                pool.indirect_dma_start(
                    out=out, out_offset=bass.IndirectOffsetOnAxis(
                        ap=frow[:, k, ID_AT:ID_AT + 1].bitcast(U32), axis=0),
                    in_=fout[:, k, :], in_offset=None, bounds_check=TOKENS - 1,
                    oob_is_err=False).then_inc(stored[k], 16)

            ffn_steps(pool, step)
            for k in range(FB):
                pool.wait_ge(stored[k], 16 * (FT // FB))

        @block.tensor
        def _(pe):
            mm = nc.tensor.matmul

            pe.wait_ge(weights_in, 64)
            for n, (left, right) in enumerate(((wqT, wkT), (wvT, wo_sb))):
                for q in range(HEADS // 4):
                    for h in (4 * q, 4 * q + 2, 4 * q + 1, 4 * q + 3):
                        r = HD * (h % 2)
                        b = banks[4 * n + 2 * (q % 2) + h % 2]
                        if h == 4 * q and q >= 2:
                            pe.wait_ge(m_copied if n else a_rest, 2 * (q - 1))
                        at = ((h // 2) % 2) * D
                        last = mm(b[:, at:at + D], left[r:r + HD, h // 2, :], right[r:r + HD, h // 2, :],
                                  start=True, stop=True, skip_group_check=True)
                    last.then_inc(fold_ready, 1)
            pe.wait_ge(consts_cast, 4)
            pe.wait_ge(a_rest, 8)
            pe.wait_ge(m_copied, 8)
            mm(MISC[:, 0:EXPERTS], ones_f[:], cent_sq[:], start=True, stop=True).then_inc(norm_ready, 1)

            def turn_x(g):
                pe.wait_ge(ln1_done, TPG * (g + 1))
                for t in range(TPG):
                    last = nc.tensor.transpose(MISC[:, t * P:(t + 1) * P], xln[:, t, :], ident[:])
                last.then_inc(xT_ready, 1)

            def queries(g, h, par):
                for n, (a, b) in enumerate(((a_hi, xT_hi), (a_lo, xT_hi), (a_hi, xT_lo))):
                    last = mm(G_BANK[h % 2][:, :], a[:, h, :], b[:], start=(n == 0), stop=(n == 2))
                last.then_inc(g_ready, 1)

            def scores(s, t, par):
                for half in range(2):
                    for b in range(2):
                        last = mm(S_BANK[t % 2][half][b * SEQ:(b + 1) * SEQ, :],
                                  ctxT[:, par, t * P + b * SEQ:t * P + (b + 1) * SEQ],
                                  gq[:, par, 8 * half:8 * half + 8, t * P + b * SEQ:t * P + (b + 1) * SEQ],
                                  start=True, stop=True, skip_group_check=True)
                last.then_inc(scores_ready, 1)

            def shift(s, b):
                pe.wait_ge(max_spread, s + 1)
                for half in range(2):
                    last = mm(S_BANK[b][half][:, :], blk_b[:], max_rows[:, b, half * HALF:(half + 1) * HALF],
                              start=False, stop=True, skip_group_check=True)
                last.then_inc(shifted, 1)

            def spread(s, b):
                pe.wait_ge(inv_spread, s + 1)
                for half in range(2):
                    last = mm(S_BANK[b][half][:, :], blk_r[:], inv_rows[:, b, half * HALF:(half + 1) * HALF],
                              start=True, stop=True)
                last.then_inc(inv_ready, 1)

            def values(s, t, par, b2):
                pe.wait_ge(probs_ready, 2 * (s + 1))
                for b in range(2):
                    for half in range(2):
                        n = 2 * b + half
                        if not (isinstance(s, int) and s == 0 and n < 2):
                            pe.wait_ge(u_out, 4 * s + n - 1)
                        mm(U_BANK[half][:, :], ctxN[b * SEQ:(b + 1) * SEQ, par, t, :],
                           probs[b * SEQ:(b + 1) * SEQ, b2, half * HALF:(half + 1) * HALF],
                           start=True, stop=True).then_inc(u_ready, 1)

            def project(s, b2):
                pe.wait_ge(u_out, 4 * (s + 1))
                for h in range(HEADS):
                    last = mm(Y_BANK[:, 0:D], ut[:, b2, h, :], m_sb[:, h, :], start=(h == 0), stop=(h == HEADS - 1))
                last.then_inc(y_ready, 1)

            def turn_normed(g, par):
                pe.wait_ge(xn_done, TPG * (g + 1))
                for t in range(TPG):
                    last = nc.tensor.transpose(MISC[:, t * P:(t + 1) * P], rows[:, par, t, 0:D], ident[:])
                last.then_inc(xnT_ready, 1)

            def dots(g):
                pe.wait_ge(xnT_out, g + 1)
                for t in range(TPG):
                    last = mm(MISC[:, t * EXPERTS:(t + 1) * EXPERTS], xnT[:, t * P:(t + 1) * P], centT[:],
                              start=True, stop=True)
                last.then_inc(dots_ready, 1)

            def ranks(g):
                pe.wait_ge(onehot_done, g + 1)
                n = TPG * EXPERTS
                mm(MISC[:, 0:n], before_b[:], onehot[:].rearrange("p t e -> p (t e)"), start=True, stop=False)
                mm(MISC[:, 0:n], ones_b[:], earlier[:].rearrange("p t e -> p (t e)"),
                   start=False, stop=True).then_inc(ranks_ready, 1)

            pe.wait_ge(norm_taken, 1)
            turn_x(0)
            pe.wait_ge(a_split, HEADS // 2)
            pe.wait_ge(xT_hi_out, 1)
            pe.wait_ge(xT_lo_out, 1)
            for h in range(HEADS):
                if h >= 2:
                    pe.wait_ge(g_out, h - 1)
                queries(0, h, 0)
            pe.wait_ge(ctxT_in, 16)
            pe.wait_ge(ctxN_in, 16)

            def group(g, par, has_prev, has_next):
                for t in range(TPG):
                    s = TPG * g + t
                    before, after = HEADS_AT[t] if has_next else ([], [])
                    if t == 3 and has_prev:
                        dots(g - 1)
                    if t == 0:
                        pe.wait_ge(g_out, HEADS * (g + 1))
                        pe.wait_ge(ctxT_in, 16 * (g + 1))
                    if t >= 2 or has_prev:
                        pe.wait_ge(probs_ready, 2 * (s - 1))
                    scores(s, t, par)
                    if t >= 1 or has_prev:
                        shift(s - 1, (t + 1) % 2)
                    if t == 1 and has_next:
                        pe.wait_ge(xT_hi_out, g + 2)
                        pe.wait_ge(xT_lo_out, g + 2)
                    for h in before:
                        heads_out(g, t, h, before, has_prev)
                        queries(g + 1, h, 1 - par)
                    if t == 2 and not has_prev:
                        pe.wait_ge(ctxN_in, 16)
                    if t == 2 and has_prev:
                        pe.wait_ge(ctxN_in, 16 * (g + 1))
                    if t >= 2:
                        values(s - 2, t - 2, par, t % 2)
                    elif has_prev:
                        values(s - 2, t + 2, 1 - par, t % 2)
                    for h in after:
                        heads_out(g, t, h, before, has_prev)
                        queries(g + 1, h, 1 - par)
                    if t >= 1 or has_prev:
                        spread(s - 1, (t + 1) % 2)
                    if t == 3 and has_prev:
                        if has_next:
                            pe.wait_ge(g_out, HEADS * (g + 2))
                        else:
                            pe.wait_ge(dots_taken, g)
                        ranks(g - 1)
                    if t >= 2 or has_prev:
                        if before:
                            pe.wait_ge(g_out, HEADS * (g + 1) + max(h for h in before + after if h % 2 == 0) + 1)
                        if not (isinstance(g, int) and s <= 2):
                            pe.wait_ge(x2_done, s - 2)
                        project(s - 2, t % 2)
                    if t == 0 and has_next:
                        if has_prev:
                            pe.wait_ge(g_out, HEADS * (g + 1))
                        turn_x(g + 1)
                    if t == 2 and has_prev:
                        if has_next:
                            pe.wait_ge(g_out, HEADS * (g + 1) + 12)
                        else:
                            pe.wait_ge(ranks_taken, g - 1)
                        turn_normed(g - 1, 1 - par)

            def heads_out(g, t, h, before, has_prev):
                first = h in HEADS_AT[t][0][:2] if h % 2 == 0 else h == min(k for k in sum(HEADS_AT[t], []) if k % 2)
                if not first:
                    pe.wait_ge(g_out, HEADS * (g + 1) + h - 1)
                elif h % 2 == 0:
                    if t == 3 or has_prev:
                        pe.wait_ge(x2_done, TPG * g + t - 2)
                    pe.wait_ge(g_out, HEADS * (g + 1) + h - 1)
                elif t == 2:
                    pe.wait_ge(g_out, HEADS * (g + 1) + h - 1)
                elif t == 3 and has_prev:
                    pe.wait_ge(dots_taken, g)

            groups(pe, group)
            s = TILES
            last = GROUPS - 1
            shift(s - 1, 1)
            values(s - 2, 2, last % 2, 0)
            spread(s - 1, 1)
            pe.wait_ge(x2_done, s - 2)
            project(s - 2, 0)
            values(s - 1, 3, last % 2, 1)
            pe.wait_ge(x2_done, s - 1)
            project(s - 1, 1)
            pe.wait_ge(ranks_taken, last)
            turn_normed(last, last % 2)
            dots(last)
            pe.wait_ge(dots_taken, last + 1)
            ranks(last)
            pe.wait_ge(ranks_taken, last + 1)
            mm(MISC[:, 0:EXPERTS], ones_b[:], seen[:], start=True, stop=True).then_inc(counts_ready, 1)

            pe.wait_ge(tiles_found, 1)
            pe.wait_ge(ffn_in, 32)

            def step(j, k, turn, static):
                b = k % 2
                if static < FT:
                    pe.wait_ge(frow_in[k], 16 * (turn + 1))
                    if static >= 2:
                        pe.wait_ge(fxT_out, j - 1)
                    nc.tensor.transpose(banks[b][:, 0:D], frow[:, k, 0:D], ident[:]).then_inc(fxT_ready, 1)
                if static >= 2:
                    pe.wait_ge(act_done, j - 1)
                    if static >= 4:
                        pe.wait_ge(actT_out, j - 3)
                    for c in range(2):
                        last = nc.tensor.transpose(banks[4 + b][:, c * P:(c + 1) * P], act[:, b, c * P:(c + 1) * P],
                                                   ident[:])
                    last.then_inc(actT_ready, 1)
                if 1 <= static <= FT:
                    e = pe.value_load(t_expert[0:1, bass.ds(j - 1, 1)], min_val=0, max_val=EXPERTS - 1)
                    pe.wait_ge(fxT_out, j)
                    if static >= 3:
                        pe.wait_ge(act_done, j - 2)
                    mm(banks[3 - b][:, :], fxT[:, 1 - b, :], upw[:, bass.ds(e * (2 * HID), 2 * HID)],
                       start=True, stop=True).then_inc(up_ready, 1)
                if static >= 2:
                    e = pe.value_load(t_expert[0:1, bass.ds(j - 2, 1)], min_val=0, max_val=EXPERTS - 1)
                    pe.wait_ge(actT_out, j - 1)
                    if static >= 4:
                        pe.wait_ge(fout_done, j - 3)
                    for c in range(2):
                        last = mm(banks[6 + b][:, 0:D], actT[:, b, c * P:(c + 1) * P],
                                  downw[:, bass.ds(e * (2 * D) + c * D, D)], start=(c == 0), stop=(c == 1))
                    last.then_inc(down_ready, 1)

            ffn_steps(pe, step)

        @block.scalar
        def _(sc):
            copy = nc.scalar.copy

            for n in range(2):
                for q in range(HEADS // 4):
                    sc.wait_ge(fold_ready, 4 * n + q + 1)
                    for r in range(2):
                        b = banks[4 * n + 2 * (q % 2) + r]
                        src = b[:, 0:2 * D].rearrange("p (k d) -> p k d", k=2)
                        if n == 0:
                            copy(a_hi[:, 4 * q + r:4 * q + r + 3:2, :], src).then_inc(a_split, 1)
                        else:
                            copy(m_sb[:, 4 * q + r:4 * q + r + 3:2, :], src).then_inc(m_copied, 1)

            def turned_x(g):
                sc.wait_ge(xT_ready, g + 1)
                copy(xT_hi[:], MISC[:]).then_inc(xT_hi_out, 1)

            def queries_out(g, h, par):
                sc.wait_ge(g_ready, HEADS * g + h + 1)
                copy(gq[:, par, h, :], G_BANK[h % 2][:]).then_inc(g_out, 1)

            def exps(s, b):
                sc.wait_ge(shifted, s + 1)
                if not (isinstance(s, int) and s < 2):
                    sc.wait_ge(u_ready, 4 * (s - 1))
                for half in range(2):
                    nc.scalar.activation(probs[:, b, half * HALF:(half + 1) * HALF], S_BANK[b][half][:],
                                         ACT.Exp, scale=SCORE_SCALE).then_inc(exp_done, 1)

            def values_out(s, b2):
                if not (isinstance(s, int) and s < 2):
                    sc.wait_ge(y_ready, s - 1)
                for b in range(2):
                    for half in range(2):
                        sc.wait_ge(u_ready, 4 * s + 2 * b + half + 1)
                        copy(ut[:, b2, 8 * half:8 * half + 8, b * SEQ:(b + 1) * SEQ],
                             U_BANK[half][:].rearrange("p (h q) -> p h q", q=SEQ)).then_inc(u_out, 1)

            def normed_out(g):
                sc.wait_ge(xnT_ready, g + 1)
                copy(xnT[:], MISC[:]).then_inc(xnT_out, 1)

            turned_x(0)
            for h in range(HEADS):
                queries_out(0, h, 0)

            def group(g, par, has_prev, has_next):
                for t in range(TPG):
                    s = TPG * g + t
                    before, after = HEADS_AT[t] if has_next else ([], [])
                    if t >= 1 or has_prev:
                        exps(s - 1, (t + 1) % 2)
                    for h in before:
                        queries_out(g + 1, h, 1 - par)
                    if t >= 2 or has_prev:
                        values_out(s - 2, t % 2)
                    for h in after:
                        queries_out(g + 1, h, 1 - par)
                    if t == 0 and has_next:
                        turned_x(g + 1)
                    if t == 2 and has_prev:
                        normed_out(g - 1)

            groups(sc, group)
            exps(TILES - 1, 1)
            values_out(TILES - 2, 0)
            values_out(TILES - 1, 1)
            normed_out(GROUPS - 1)

            def step(j, k, turn, static):
                b = k % 2
                if static < FT:
                    sc.wait_ge(fxT_ready, j + 1)
                    if static >= 2:
                        sc.wait_ge(up_ready, j - 1)
                    copy(fxT[:, b, :], banks[b][:, 0:D]).then_inc(fxT_out, 1)
                if static >= 2:
                    sc.wait_ge(actT_ready, j - 1)
                    if static >= 4:
                        sc.wait_ge(down_ready, j - 3)
                    copy(actT[:, b, :], banks[4 + b][:, 0:HID]).then_inc(actT_out, 1)
                if 1 <= static <= FT:
                    sc.wait_ge(up_ready, j)
                    if static >= 3:
                        sc.wait_ge(act_done, j - 2)
                    nc.scalar.activation(gate[:, 1 - b, :], banks[3 - b][:, HID:2 * HID], ACT.Silu).then_inc(gated, 1)

            ffn_steps(sc, step)

        @block.vector
        def _(dve):
            v = nc.vector
            seq = Chain(dve, dve_seq)

            dve.wait_ge(small_in, 32)
            v.tensor_tensor(cent_sq[:], centT[:], centT[:], ALU.mult).then_inc(consts_cast, 1)
            dve.wait_ge(consts_made, 2)
            seq.mark(v.tensor_copy(id32b[:], id32f[:]))
            seq.mark(v.tensor_copy(blk_b[:], blk_f[:]))
            seq.mark(v.tensor_copy(blk_r[:], blk_f[:]))
            seq.mark(v.tensor_copy(ones_b[:], ones_f[:]))
            seq.wait()
            v.memset(key_max2[:], 0.0).then_inc(consts_cast, 1)
            v.memset(key_sum2[:], 0.0).then_inc(consts_cast, 1)
            v.memset(square[:], 0.0).then_inc(consts_cast, 1)

            def statistics(src, stats, mv):
                for t in range(TPG):
                    seq.mark(v.bn_stats(stats[:, t, :], src[:, t, :]))
                seq.wait()
                settle_v()
                for t in range(TPG):
                    seq.mark(v.bn_aggr(mv[:, t, :], stats[:, t, :]))
                seq.wait()

            def measure_x(g):
                dve.wait_ge(x_in, 16 * (g + 1))
                statistics(xin, stats1, mv1)
                v.tensor_scalar(var1[:], mv1[:, :, 1], LN_EPS, None, ALU.add).then_inc(var1_done, 1)

            def norm_x(g):
                dve.wait_ge(rstd1_done, g + 1)
                if not (isinstance(g, int) and g == 0):
                    dve.wait_ge(xT_ready, g)
                for t in range(TPG):
                    v.tensor_scalar(xln[:, t, :], xin[:, t, :], mv1[:, t, 0:1], rstd1[:, t:t + 1],
                                    ALU.subtract, ALU.mult).then_inc(ln1_done, 1)

            def split_x(g):
                dve.wait_ge(xT_hi_out, g + 1)
                v.tensor_tensor(xT_lo[:], MISC[:], xT_hi[:].bitcast(F32), ALU.subtract).then_inc(xT_lo_out, 1)

            def across_halves(dst, src):
                for q in range(P // BLK):
                    seq.mark(v.tensor_copy(dst[q * BLK:(q + 1) * BLK, :], src[(q ^ 1) * BLK:((q ^ 1) + 1) * BLK, :]))
                seq.wait()

            def maxima(s, b):
                dve.wait_ge(scores_ready, s + 1)
                for half in range(2):
                    seq.mark(v.transpose(turned[:, half * HALF:(half + 1) * HALF], S_BANK[b][half][:]))
                seq.wait()
                seq.then(v.tensor_reduce(key_max[:], turned[:].rearrange("p (b k) -> p b k", k=BLK), AX_X, ALU.max))
                across_halves(key_max2, key_max)
                seq.then(v.tensor_tensor(top[:], key_max[:], key_max2[:], ALU.max))
                if not (isinstance(s, int) and s < 2):
                    dve.wait_ge(max_spread, s - 1)
                v.tensor_scalar(neg_max[:, b], top[:], -1.0, None, ALU.mult).then_inc(max_found, 1)
                dve.wait_ge(max_found, 3 * s + 1)
                for q in (1, 3):
                    r = slice(q * BLK, (q + 1) * BLK)
                    v.scalar_tensor_tensor(out=neg_max[r, b], in0=top[r, :], scalar=-1.0, in1=neg_max[r, b],
                                           op0=ALU.mult, op1=ALU.subtract).then_inc(max_found, 1)

            def sums(s, b):
                dve.wait_ge(exp_done, 2 * (s + 1))
                seq.then(v.transpose(turned_p[:], probs[:, b, :]))
                seq.then(v.tensor_reduce(key_sum[:], turned_p[:].rearrange("p (b k) -> p b k", k=BLK), AX_X, ALU.add))
                across_halves(key_sum2, key_sum)
                seq.then(v.tensor_tensor(total[:], key_sum[:], key_sum2[:], ALU.add))
                if not (isinstance(s, int) and s < 2):
                    dve.wait_ge(inv_spread, s - 1)
                seq.then(v.reciprocal(inv[:, b], total[:]))
                seq.then(v.tensor_copy(inv_hi[:], inv[:, b]))
                for q in (1, 3):
                    r = slice(q * BLK, (q + 1) * BLK)
                    v.tensor_tensor(inv[r, b], inv[r, b], inv_hi[r, :].bitcast(F32),
                                    ALU.subtract).then_inc(inv_found, 1)

            def normalise(s, b):
                dve.wait_ge(inv_ready, s + 1)
                for half in range(2):
                    r = slice(half * HALF, (half + 1) * HALF)
                    v.tensor_tensor(probs[:, b, r], probs[:, b, r], S_BANK[b][half][:],
                                    ALU.mult).then_inc(probs_ready, 1)

            def add_residual(s, t, par):
                dve.wait_ge(y_ready, s + 1)
                if t == 0:
                    if not (isinstance(s, int) and s == 0):
                        dve.wait_ge(base_done, 3 * div4(s))
                dve.wait_ge(xres_in, 16 * (div4(s - t) + 1))
                v.tensor_tensor(x2[:, t, :], Y_BANK[:, 0:D], xres[:, par, t, :], ALU.add).then_inc(x2_done, 1)

            def measure_x2(g):
                dve.wait_ge(x2_done, TPG * (g + 1))
                statistics(x2, stats2, mv2)
                var = mv2[:, :, 1]
                seq.then(v.tensor_scalar(spread2[:, 0, :], var, LN_EPS, None, ALU.add))
                seq.then(v.reciprocal(var_inv[:], spread2[:, 0, :]))
                seq.then(v.tensor_tensor(var_inv[:], var, var_inv[:], ALU.mult))
                v.tensor_scalar(spread2[:, 1, :], var_inv[:], RMS_EPS, None, ALU.add).then_inc(spread2_done, 1)

            def norm_x2(g, par):
                dve.wait_ge(root2_done, g + 1)
                for t in range(TPG):
                    v.tensor_scalar(xl[:, t, :], x2[:, t, :], mv2[:, t, 0:1], root2[:, 0, t:t + 1],
                                    ALU.subtract, ALU.mult).then_inc(xl_done, 1)
                dve.wait_ge(xl_done, TPG * (g + 1))
                dve.wait_ge(scattered, 16 * (TPG * g + 1))
                for t in range(TPG):
                    v.scalar_tensor_tensor(out=rows[:, par, t, 0:D], in0=xl[:, t, :], scalar=root2[:, 1, t:t + 1],
                                           in1=scale_b[:], op0=ALU.mult, op1=ALU.mult).then_inc(xn_done, 1)
                dve.wait_ge(xn_done, TPG * (g + 1))
                for t in range(TPG):
                    seq.mark(v.tensor_tensor_reduce(square[:, t, :], rows[:, par, t, 0:D], rows[:, par, t, 0:D], 1.0, 0.0,
                                                    ALU.mult, ALU.add, norm2[:, t:t + 1]))
                seq.wait()
                seq.then(v.tensor_tensor(norms[:], norm2[:].unsqueeze(2).to_broadcast([P, TPG, EXPERTS]),
                                         cent_norm[:].unsqueeze(1).to_broadcast([P, TPG, EXPERTS]), ALU.add))

            def choose(g):
                def experts(ap):
                    return ap.unsqueeze(1).to_broadcast([P, TPG, EXPERTS])

                dve.wait_ge(dots_ready, g + 1)
                v.scalar_tensor_tensor(out=dist[:].rearrange("p t e -> p (t e)"), in0=MISC[:, 0:TPG * EXPERTS],
                                       scalar=-2.0, in1=norms[:].rearrange("p t e -> p (t e)"), op0=ALU.mult,
                                       op1=ALU.add).then_inc(dots_taken, 1)
                dve.wait_ge(dots_taken, g + 1)
                seq.then(v.tensor_reduce(least[:], dist[:], AX_X, ALU.min))
                seq.then(v.tensor_tensor(cand[:], dist[:], least[:].unsqueeze(2).to_broadcast([P, TPG, EXPERTS]),
                                         ALU.is_le))
                seq.then(v.tensor_tensor(cand[:], cand[:], experts(expert_m8[:]), ALU.mult))
                seq.then(v.tensor_reduce(chosen[:], cand[:], AX_X, ALU.min))
                seq.then(v.tensor_tensor(onehot[:], experts(expert_m8[:]),
                                         chosen[:].unsqueeze(2).to_broadcast([P, TPG, EXPERTS]), ALU.is_equal))
                seq.then(v.tensor_copy(earlier[:, 0, :], seen[:]))
                for t in range(1, TPG):
                    seq.then(v.tensor_tensor(earlier[:, t, :], earlier[:, t - 1, :], onehot[:, t - 1, :], ALU.add))
                v.tensor_tensor(seen[:], earlier[:, TPG - 1, :], onehot[:, TPG - 1, :],
                                ALU.add).then_inc(onehot_done, 1)

            def places(g, par):
                dve.wait_ge(ranks_ready, g + 1)
                v.tensor_tensor(place[:], MISC[:, 0:TPG * EXPERTS].rearrange("p (t e) -> p t e", e=EXPERTS),
                                region_of[:].unsqueeze(1).to_broadcast([P, TPG, EXPERTS]),
                                ALU.add).then_inc(ranks_taken, 1)
                dve.wait_ge(ranks_taken, g + 1)
                seq.then(v.tensor_tensor(place[:], place[:], onehot[:], ALU.mult))
                seq.then(v.tensor_reduce(place_f[:], place[:], AX_X, ALU.add))
                v.tensor_copy(place_u[:, par, :], place_f[:]).then_inc(place_done, 1)

            for q in range(HEADS // 4):
                dve.wait_ge(a_split, 2 * q + 2)
                for r in range(2):
                    b = banks[2 * (q % 2) + r]
                    v.tensor_tensor(a_lo[:, 4 * q + r:4 * q + r + 3:2, :],
                                    b[:, 0:2 * D].rearrange("p (k d) -> p k d", k=2),
                                    a_hi[:, 4 * q + r:4 * q + r + 3:2, :].bitcast(F32),
                                    ALU.subtract).then_inc(a_rest, 1)
            measure_x(0)
            norm_x(0)
            dve.wait_ge(norm_ready, 1)
            v.tensor_copy(cent_norm[:], MISC[:, 0:EXPERTS]).then_inc(norm_taken, 1)
            split_x(0)

            group_of = {}

            def div4(s):
                return group_of["g"] if True else s

            def group(g, par, has_prev, has_next):
                for t in range(TPG):
                    s = TPG * g + t
                    if t == 1 and has_next:
                        split_x(g + 1)
                    if t == 3:
                        group_of["g"] = g
                        add_residual(s - 3, 0, par)
                    elif has_prev:
                        group_of["g"] = g - 1
                        add_residual(s - 3, t + 1, 1 - par)
                    if t == 3 and has_prev:
                        choose(g - 1)
                    if t == 0 and has_next:
                        measure_x(g + 1)
                    if t == 2 and has_prev:
                        measure_x2(g - 1)
                    maxima(s, t % 2)
                    if t == 0 and has_next:
                        norm_x(g + 1)
                    if t >= 1 or has_prev:
                        sums(s - 1, (t + 1) % 2)
                    if t == 2 and has_prev:
                        norm_x2(g - 1, 1 - par)
                    if t >= 1 or has_prev:
                        normalise(s - 1, (t + 1) % 2)
                    if t == 3 and has_prev:
                        places(g - 1, 1 - par)

            group(0, 0, False, True)
            with dve.Fori(0, LOOPS) as i:
                seq.loop(i, DVE_PER_TURN)
                for k in range(2):
                    group(1 + k + 2 * i, (1 + k) % 2, True, True)
                seq.end_loop(LOOPS)
            last = GROUPS - 1
            group(last, last % 2, True, False)
            group_of["g"] = last
            add_residual(TILES - 3, 1, last % 2)
            sums(TILES - 1, 1)
            normalise(TILES - 1, 1)
            add_residual(TILES - 2, 2, last % 2)
            add_residual(TILES - 1, 3, last % 2)
            measure_x2(last)
            norm_x2(last, last % 2)
            choose(last)
            places(last, last % 2)

            dve.wait_ge(counts_ready, 1)
            seq.then(v.tensor_copy(count[:], MISC[:, 0:EXPERTS]))
            seq.mark(v.tensor_tensor(pad_at[:], count[:], region_of[:], ALU.add))
            seq.then(v.tensor_scalar(count_i[:], count[:], float(P - 1), None, ALU.add))
            seq.mark(v.tensor_scalar(count_i[:], count_i[:], P.bit_length() - 1, None, ALU.logical_shift_right))
            seq.wait()
            v.tensor_scalar(pad_u[:], pad_at[:], part_f[:, 0:1], None, ALU.add).then_inc(pads_found, 1)
            seq.then(v.tensor_copy(ntile[:], count_i[:]))
            seq.then(v.tensor_tensor(upto[:], upto[:], ntile[:].unsqueeze(1).to_broadcast([P, EXPERTS, EXPERTS]),
                                     ALU.mult))
            seq.then(v.tensor_reduce(cumul[:], upto[:], AX_X, ALU.add))
            seq.then(v.tensor_tensor(done[:], tile_no[:].unsqueeze(2).to_broadcast([P, FT, EXPERTS]),
                                     cumul[:].unsqueeze(1).to_broadcast([P, FT, EXPERTS]), ALU.is_ge))
            seq.mark(v.tensor_reduce(tile_e[:], done[:], AX_X, ALU.add))
            seq.then(v.tensor_tensor(done_n[:], done[:], ntile[:].unsqueeze(1).to_broadcast([P, FT, EXPERTS]),
                                     ALU.mult))
            seq.then(v.tensor_reduce(tile_b[:], done_n[:], AX_X, ALU.add))
            seq.then(v.tensor_tensor(tile_b[:], tile_no[:], tile_b[:], ALU.subtract))
            seq.mark(v.tensor_scalar(tile_r[:], tile_e[:], float(REGION), None, ALU.mult))
            seq.then(v.tensor_scalar(tile_e[:], tile_e[:], float(EXPERTS - 1), None, ALU.min))
            seq.then(v.scalar_tensor_tensor(out=tile_r[:], in0=tile_b[:], scalar=float(P), in1=tile_r[:],
                                            op0=ALU.mult, op1=ALU.add))
            seq.mark(v.tensor_copy(t_expert[:], tile_e[:]))
            seq.then(v.tensor_copy(t_row[:], tile_r[:]))
            v.memset(spare_v[:], 0.0).then_inc(tiles_found, 1)

            def step(j, k, turn, static):
                b = k % 2
                if 1 <= static <= FT:
                    dve.wait_ge(gated, j)
                    if static >= 3:
                        dve.wait_ge(actT_ready, j - 2)
                    v.tensor_tensor(act[:, 1 - b, :], gate[:, 1 - b, :], banks[3 - b][:, 0:HID],
                                    ALU.mult).then_inc(act_done, 1)
                if static >= 2:
                    k2 = (k - 2) % FB
                    dve.wait_ge(down_ready, j - 1)
                    v.tensor_tensor(fout[:, k2, :], banks[6 + b][:, 0:D], frow[:, k2, D:2 * D],
                                    ALU.add).then_inc(fout_done, 1)

            ffn_steps(dve, step)


DVE_PER_TURN = 206


def kernel(x, ctx_1024, L0_xattn_Wq, L0_xattn_Wk, L0_xattn_Wv, L0_xattn_Wo, L0_ffn_scale, L0_ffn_centroids,
           L0_ffn_up_w, L0_ffn_down_w):
    import numpy as np
    from concourse import bacc
    from concourse.bass_utils import run_bass_kernel_spmd

    def lay(a):
        return np.ascontiguousarray(a)

    flat = np.asarray(ctx_1024).reshape(TOKENS, D)
    arrays = {
        "x": lay(np.asarray(x).reshape(TOKENS, D)),
        "ctx": lay(flat),
        "ctx_t": lay(flat.T),
        "wq_t": lay(np.asarray(L0_xattn_Wq).T),
        "wk_t": lay(np.asarray(L0_xattn_Wk).T),
        "wv_t": lay(np.asarray(L0_xattn_Wv).T),
        "wo": lay(L0_xattn_Wo),
        "scale": lay(np.asarray(L0_ffn_scale).reshape(1, D)),
        "cent_t": lay(np.asarray(L0_ffn_centroids).T),
        "up_w": lay(L0_ffn_up_w),
        "down_w": lay(L0_ffn_down_w),
    }
    nc = bacc.Bacc("TRN2", target_bir_lowering=False, num_devices=1)
    args = [nc.dram_tensor(n, a.shape, mybir.dt.from_np(a.dtype), kind="ExternalInput").ap()
            for n, a in arrays.items()]
    out = nc.dram_tensor("out", (TOKENS, D), F32, kind="ExternalOutput").ap()
    xattn_ffn(nc, *args, out)
    r = run_bass_kernel_spmd(nc, [arrays], core_ids=[0])
    return r.results[0]["out"].reshape(TOKENS // SEQ, SEQ, D)
```

```python
from contextlib import ExitStack

import concourse.bass as bass
from concourse import mybir

F32 = mybir.dt.float32
F32R = mybir.dt.float32r
BF16 = mybir.dt.bfloat16
U32 = mybir.dt.uint32
I32 = mybir.dt.int32
ALU = mybir.AluOpType
ACT = mybir.ActivationFunctionType
AX_X = mybir.AxisListType.X

P = 128
D = 128
SEQ = 64
TOKENS = 4096
HEADS = 16
HD = 64
TILES = TOKENS // P
TPG = 4
GROUPS = TILES // TPG
GT = TPG * P
HALF = HEADS // 2 * SEQ
BLK = 32
NBLK = HEADS * SEQ // BLK
SCORE_SCALE = HD ** -0.5
LN_EPS = 1e-5
RMS_EPS = 1e-6

EXPERTS = 8
HID = 256
ROW = 2 * D + 4
ID_AT = 2 * D
REGION = TOKENS + P
NO_TOKEN = 1 << 20
FT = 40
FB = 8
HEADS_AT = [[[], [], [], []], [[0], [1, 2], [3, 4], [5]], [[6], [7, 8], [9], [10]], [[11], [12, 13], [14], [15]]]
MISC_HEADS = (1, 3, 5, 6, 8, 10, 11, 13, 15)
LOOPS = (GROUPS - 2) // 2


def xattn_ffn(nc, x, ctx, ctx_t, wq_t, wk_t, wv_t, wo, scale, cent_t, up_w, down_w, out):
    x_v = x.rearrange("(g t p) d -> g p t d", t=TPG, p=P)
    ctx_v = ctx.rearrange("(g t p) d -> g p t d", t=TPG, p=P)
    ctxt_v = ctx_t.rearrange("d (g n) -> g d n", g=GROUPS)
    table = nc.dram_tensor("sorted_rows", (EXPERTS * REGION + FT * P, ROW), F32)

    with ExitStack() as es:
        def sb(name, shape, dt=F32):
            return es.enter_context(nc.sbuf_tensor(name, shape, dt))

        def sem(name):
            return es.enter_context(nc.semaphore(name))

        banks = [es.enter_context(nc.psum_tensor(f"bank{i}", [P, 512], F32)) for i in range(8)]
        S_BANK = [banks[0:2], banks[2:4]]
        Y_BANK, MISC = banks[4], banks[5]
        U_BANK, R_BANK = banks[6], banks[7]
        TURN_BANK, UP_BANK, ACT_BANK, DOWN_BANK = banks[0], banks[2:4], banks[4:6], banks[6:8]

        a_hi = sb("a_hi", [P, HEADS, D], F32R)
        a_lo = sb("a_lo", [P, HEADS, D], F32R)
        m_sb = sb("m_sb", [P, HEADS, D])
        upw = sb("upw", [P, EXPERTS * 2 * HID])
        downw = sb("downw", [P, EXPERTS * 2 * D])
        scale_b = sb("scale_b", [P, D])
        centT = sb("centT", [P, EXPERTS])
        cent_sq = sb("cent_sq", [P, EXPERTS])
        cent_norm = sb("cent_norm", [P, EXPERTS])
        ident = sb("ident", [P, P])
        id32f = sb("id32f", [P, BLK])
        id32b = sb("id32b", [P, BLK], BF16)
        blk_f = sb("blk_f", [P, P])
        blk_b = sb("blk_b", [P, P], BF16)
        blk_r = sb("blk_r", [P, P], F32R)
        ones_f = sb("ones_f", [P, P])
        ones_b = sb("ones_b", [P, P], BF16)
        before_b = sb("before_b", [P, P], BF16)
        expert_m8 = sb("expert_m8", [P, EXPERTS])
        region_of = sb("region_of", [P, EXPERTS])

        xin = sb("xin", [P, TPG, D])
        xres = sb("xres", [P, 2, TPG, D])
        ctxT = sb("ctxT", [P, 2, GT])
        ctxN = sb("ctxN", [P, 2, TPG, D])
        stats1 = sb("stats1", [P, TPG, 6])
        mv1 = sb("mv1", [P, TPG, 2])
        var1 = sb("var1", [P, TPG])
        rstd1 = sb("rstd1", [P, TPG])
        xln = sb("xln", [P, TPG, D])
        xT_hi = sb("xT_hi", [P, GT], F32R)
        xT_lo = sb("xT_lo", [P, GT], F32R)
        gq = sb("gq", [P, 2, HEADS, GT])
        turned = sb("turned", [P, 2 * HALF])
        turned_p = sb("turned_p", [P, 2 * HALF])
        key_max = sb("key_max", [P, NBLK])
        key_max2 = sb("key_max2", [P, NBLK])
        top = sb("top", [P, NBLK])
        neg_max = sb("neg_max", [P, 2, NBLK], BF16)
        max_rows = sb("max_rows", [P, 2, 2 * HALF], BF16)
        probs = sb("probs", [P, 2, 2 * HALF])
        key_sum = sb("key_sum", [P, NBLK])
        key_sum2 = sb("key_sum2", [P, NBLK])
        total = sb("total", [P, NBLK])
        inv = sb("inv", [P, 2, NBLK])
        inv_hi = sb("inv_hi", [P, NBLK], F32R)
        inv_rows = sb("inv_rows", [P, 2, 2 * HALF], F32R)
        ut = sb("ut", [P, 2, HEADS, P])
        weights = ut[:].rearrange("p a (b h) d -> p (a b) h d", b=2)
        wqT, wkT, wvT, wo_sb = (weights[:, n] for n in range(4))
        x2 = sb("x2", [P, TPG, D])
        stats2 = sb("stats2", [P, TPG, 6])
        mv2 = sb("mv2", [P, TPG, 2])
        spread2 = sb("spread2", [P, 2, TPG])
        var_inv = sb("var_inv", [P, TPG])
        root2 = sb("root2", [P, 2, TPG])
        power = sb("power", [P, 2 * TPG])
        xl = sb("xl", [P, TPG, D])
        square = sb("square", [P, TPG, D])
        norm2 = sb("norm2", [P, TPG])
        rows = sb("rows", [P, 2, TPG, ROW])
        xnT = sb("xnT", [P, GT])
        norms = sb("norms", [P, TPG, EXPERTS])
        dist = sb("dist", [P, TPG, EXPERTS])
        least = sb("least", [P, TPG])
        cand = sb("cand", [P, TPG, EXPERTS])
        chosen = sb("chosen", [P, TPG])
        onehot = sb("onehot", [P, TPG, EXPERTS], BF16)
        earlier = sb("earlier", [P, TPG, EXPERTS], BF16)
        seen = sb("seen", [P, EXPERTS], BF16)
        place = sb("place", [P, TPG, EXPERTS])
        place_f = sb("place_f", [P, TPG])
        place_u = sb("place_u", [P, 2, TPG], U32)
        token_f = sb("token_f", [P, TPG])

        count = sb("count", [P, EXPERTS])
        count_i = sb("count_i", [P, EXPERTS], I32)
        ntile = sb("ntile", [P, EXPERTS])
        upto = sb("upto", [P, EXPERTS, EXPERTS])
        cumul = sb("cumul", [P, EXPERTS])
        pad_at = sb("pad_at", [P, EXPERTS])
        pad_u = sb("pad_u", [P, EXPERTS], U32)
        part_f = sb("part_f", [P, 1])
        pad_row = sb("pad_row", [P, ROW])
        tile_no = sb("tile_no", [P, FT])
        done = sb("done", [P, FT, EXPERTS])
        done_n = sb("done_n", [P, FT, EXPERTS])
        tile_e = sb("tile_e", [P, FT])
        tile_b = sb("tile_b", [P, FT])
        tile_r = sb("tile_r", [P, FT])
        t_expert = sb("t_expert", [P, FT], I32)
        t_row = sb("t_row", [P, FT], I32)

        spare_v = sb("spare_v", [P, 1])
        spare_p = sb("spare_p", [P, 3])
        room = gq[:, 0].rearrange("p h n -> p (h n)")
        taken = [0]

        def from_queries(shape):
            n = shape[0] * shape[1]
            taken[0] += n
            return room[:, taken[0] - n:taken[0]].rearrange("p (a b) -> p a b", a=shape[0])

        frow = from_queries([FB, ROW])
        fxT = from_queries([1, 2 * P])[:, 0]
        gate = from_queries([2, HID])
        act = from_queries([2, HID])
        actT = from_queries([2, HID])
        fout = from_queries([FB, D])

        weights_in = sem("weights_in")
        ffn_in = sem("ffn_in")
        small_in = sem("small_in")
        x_in = sem("x_in")
        xres_in = sem("xres_in")
        ctxT_in = sem("ctxT_in")
        ctxN_in = sem("ctxN_in")
        pool_seq = sem("pool_seq")
        consts_made = sem("consts_made")
        dve_seq = sem("dve_seq")
        consts_cast = sem("consts_cast")
        fold_ready = sem("fold_ready")
        a_rest = sem("a_rest")
        m_copied = sem("m_copied")
        a_split = sem("a_split")
        norm_ready = sem("norm_ready")
        norm_taken = sem("norm_taken")
        var1_done = sem("var1_done")
        rstd1_done = sem("rstd1_done")
        spread2_done = sem("spread2_done")
        root2_done = sem("root2_done")
        ln1_done = sem("ln1_done")
        xT_ready = sem("xT_ready")
        xT_hi_out = sem("xT_hi_out")
        xT_lo_out = sem("xT_lo_out")
        g_ready = sem("g_ready")
        g_out = sem("g_out")
        scores_ready = sem("scores_ready")
        max_found = sem("max_found")
        max_spread = sem("max_spread")
        shifted = sem("shifted")
        exp_done = sem("exp_done")
        inv_found = sem("inv_found")
        inv_spread = sem("inv_spread")
        inv_ready = sem("inv_ready")
        probs_ready = sem("probs_ready")
        u_ready = sem("u_ready")
        u_out = sem("u_out")
        y_ready = sem("y_ready")
        x2_done = sem("x2_done")
        xl_done = sem("xl_done")
        base_done = sem("base_done")
        xn_done = sem("xn_done")
        xnT_ready = sem("xnT_ready")
        xnT_out = sem("xnT_out")
        dots_ready = sem("dots_ready")
        dots_taken = sem("dots_taken")
        onehot_done = sem("onehot_done")
        ranks_ready = sem("ranks_ready")
        ranks_taken = sem("ranks_taken")
        place_done = sem("place_done")
        scattered = sem("scattered")
        counts_ready = sem("counts_ready")
        pads_found = sem("pads_found")
        padded = sem("padded")
        tiles_found = sem("tiles_found")
        frow_in = [sem(f"frow{k}_in") for k in range(FB)]
        fxT_ready = sem("fxT_ready")
        fxT_out = sem("fxT_out")
        up_ready = sem("up_ready")
        gated = sem("gated")
        act_done = sem("act_done")
        actT_ready = sem("actT_ready")
        actT_out = sem("actT_out")
        down_ready = sem("down_ready")
        fout_done = sem("fout_done")
        settled = sem("settled")
        stored = [sem(f"out{k}_stored") for k in range(FB)]

        block = es.enter_context(nc.Block())

        def g_bank(h):
            return MISC if h in MISC_HEADS else Y_BANK

        def groups(eng, group):
            group(0, 0, False, True)
            with eng.Fori(0, LOOPS) as i:
                for k in range(2):
                    group(1 + k + 2 * i, (1 + k) % 2, True, True)
            group(GROUPS - 1, (GROUPS - 1) % 2, True, False)

        def ffn_pairs(eng, pair):
            for k in range(0, FB, 2):
                pair(k, k, 0, k)
            with eng.Fori(1, FT // FB) as i:
                for k in range(0, FB, 2):
                    pair(FB * i + k, k, i, FB + k)

        def settle_v():
            return nc.vector.memset(spare_v[:], 0.0)

        def settle_p(column):
            return nc.gpsimd.tensor_tensor(spare_p[:, column:column + 1], part_f[:], part_f[:], ALU.add)

        class Chain:

            def __init__(self, eng, sem):
                self.eng, self.sem, self.base, self.n = eng, sem, 0, 0

            def mark(self, ins):
                ins.then_inc(self.sem, 1)
                self.n += 1

            def wait(self):
                self.eng.wait_ge(self.sem, self.base + self.n)

            def then(self, ins):
                self.mark(ins)
                self.wait()

            def loop(self, i, per_turn):
                self.start = self.n
                self.base, self.n = self.n + i * per_turn, 0
                self.per_turn = per_turn

            def end_loop(self, turns):
                assert self.n == self.per_turn, (self.n, self.per_turn)
                self.base, self.n = 0, self.start + turns * self.per_turn

        @block.sync
        def _(sp):
            sp.dma_start(wqT, wq_t.rearrange("(c p) d -> p c d", p=P)).then_inc(weights_in, 16)
            sp.dma_start(wkT, wk_t.rearrange("(c p) d -> p c d", p=P)).then_inc(weights_in, 16)
            sp.dma_start(wvT, wv_t.rearrange("(c p) d -> p c d", p=P)).then_inc(weights_in, 16)
            sp.dma_start(wo_sb, wo.rearrange("(c p) d -> p c d", p=P)).then_inc(weights_in, 16)
            sp.dma_start(xin[:], x_v[0]).then_inc(x_in, 16)
            sp.dma_start(ctxT[:, 0, :], ctxt_v[0]).then_inc(ctxT_in, 16)
            sp.dma_start(ctxN[:, 0], ctx_v[0]).then_inc(ctxN_in, 16)
            sp.dma_start(xres[:, 0], x_v[0]).then_inc(xres_in, 16)
            sp.dma_start(scale_b[:], scale.to_broadcast([P, D])).then_inc(small_in, 16)
            sp.dma_start(centT[:], cent_t).then_inc(small_in, 16)
            sp.dma_start(upw[:].rearrange("p (e h) -> p e h", e=EXPERTS),
                         up_w.rearrange("e d h -> d e h")).then_inc(ffn_in, 16)
            sp.dma_start(downw[:].rearrange("p (e c d) -> p e c d", e=EXPERTS, c=2),
                         down_w.rearrange("e (c p) d -> p e c d", p=P)).then_inc(ffn_in, 16)

            def group(g, par, has_prev, has_next):
                if not has_next:
                    return
                sp.wait_ge(ln1_done, TPG * (g + 1))
                sp.dma_start(xin[:], x_v[g + 1]).then_inc(x_in, 16)
                sp.wait_ge(ctxT_in, 16 * (g + 1))
                if has_prev:
                    sp.wait_ge(x2_done, TPG * g)
                sp.dma_start(ctxT[:, 1 - par, :], ctxt_v[g + 1]).then_inc(ctxT_in, 16)
                sp.wait_ge(ctxN_in, 16 * (g + 1))
                sp.dma_start(ctxN[:, 1 - par], ctx_v[g + 1]).then_inc(ctxN_in, 16)
                sp.wait_ge(xres_in, 16 * (g + 1))
                sp.dma_start(xres[:, 1 - par], x_v[g + 1]).then_inc(xres_in, 16)

            groups(sp, group)

            sp.wait_ge(tiles_found, 1)
            sp.wait_ge(padded, 16 * EXPERTS)
            sp.wait_ge(scattered, 16 * (TILES + 1))

            def pair(j, k, turn, static):
                for n in range(2):
                    if static >= FB:
                        sp.wait_ge(stored[k + n], 16 * turn)
                    row = sp.value_load(t_row[0:1, bass.ds(j + n, 1)], min_val=0,
                                        max_val=EXPERTS * REGION + (FT - 1) * P)
                    sp.dma_start(frow[:, k + n, :], table[bass.ds(row, P), :]).then_inc(frow_in[k + n], 16)

            ffn_pairs(sp, pair)

        @block.gpsimd
        def _(pool):
            seq = Chain(pool, pool_seq)
            nc.gpsimd.memset(ones_f[:], 1.0).then_inc(pool_seq, 1)
            nc.gpsimd.memset(ident[:], 0.0).then_inc(pool_seq, 1)
            nc.gpsimd.memset(id32f[:], 0.0).then_inc(pool_seq, 1)
            nc.gpsimd.memset(blk_f[:], 0.0).then_inc(pool_seq, 1)
            nc.gpsimd.memset(pad_row[:], 0.0).then_inc(pool_seq, 1)
            nc.gpsimd.memset(rows[:], 0.0).then_inc(pool_seq, 1)
            seq.n = 6
            seq.wait()
            seq.mark(nc.gpsimd.affine_select(out=ident[:], in_=ident[:], compare_op=ALU.not_equal, fill=1.0,
                                             base=0, pattern=[[-1, P]], channel_multiplier=1))
            for q in range(P // BLK):
                seq.then(nc.gpsimd.affine_select(out=id32f[:], in_=id32f[:], compare_op=ALU.not_equal, fill=1.0,
                                                 base=-BLK * q, pattern=[[-1, BLK]], channel_multiplier=1))
            for q in range(P // SEQ):
                seq.then(nc.gpsimd.memset(blk_f[q * SEQ:(q + 1) * SEQ, q * SEQ:(q + 1) * SEQ], 1.0))
            seq.mark(nc.gpsimd.iota(expert_m8[:], pattern=[[1, EXPERTS]], base=-EXPERTS, channel_multiplier=0,
                                    allow_small_or_imprecise_dtypes=True))
            seq.mark(nc.gpsimd.iota(region_of[:], pattern=[[REGION, EXPERTS]], base=0, channel_multiplier=0,
                                    allow_small_or_imprecise_dtypes=True))
            seq.mark(nc.gpsimd.iota(token_f[:], pattern=[[P, TPG]], base=0, channel_multiplier=1,
                                    allow_small_or_imprecise_dtypes=True))
            seq.mark(nc.gpsimd.iota(part_f[:], pattern=[[0, 1]], base=0, channel_multiplier=1,
                                    allow_small_or_imprecise_dtypes=True))
            seq.mark(nc.gpsimd.iota(tile_no[:], pattern=[[1, FT]], base=0, channel_multiplier=0,
                                    allow_small_or_imprecise_dtypes=True))
            seq.mark(nc.gpsimd.iota(pad_row[:, ID_AT:ID_AT + 1].bitcast(I32), pattern=[[0, 1]], base=NO_TOKEN,
                                    channel_multiplier=0))
            seq.mark(nc.gpsimd.memset(upto[:], 1.0))
            seq.mark(nc.gpsimd.memset(before_b[:], 1.0))
            seq.wait()
            seq.mark(nc.gpsimd.affine_select(out=upto[:], in_=upto[:], compare_op=ALU.is_ge, fill=0.0, base=0,
                                             pattern=[[1, EXPERTS], [-1, EXPERTS]], channel_multiplier=0))
            seq.mark(nc.gpsimd.affine_select(out=before_b[:], in_=before_b[:], compare_op=ALU.is_gt, fill=0.0,
                                             base=0, pattern=[[1, P]], channel_multiplier=-1))
            seq.wait()
            nc.gpsimd.memset(power[:], -0.5).then_inc(consts_made, 1)
            nc.gpsimd.memset(seen[:], 0.0).then_inc(consts_made, 1)
            pool.dma_start(table[EXPERTS * REGION:, :].rearrange("(t p) r -> p t r", p=P),
                           pad_row[:].unsqueeze(1).to_broadcast([P, FT, ROW])).then_inc(scattered, 16)
            pool.wait_ge(consts_cast, 4)

            pool.wait_ge(consts_made, 2)

            def root_x(g):
                pool.wait_ge(var1_done, g + 1)
                nc.gpsimd.tensor_tensor(rstd1[:], var1[:], power[:, 0:TPG], ALU.pow).then_inc(rstd1_done, 1)

            def root_x2(g):
                pool.wait_ge(spread2_done, g + 1)
                nc.gpsimd.tensor_tensor(root2[:].rearrange("p a t -> p (a t)"),
                                        spread2[:].rearrange("p a t -> p (a t)"), power[:],
                                        ALU.pow).then_inc(root2_done, 1)

            def spread_max(s, par):
                pool.wait_ge(max_found, 3 * (s + 1))
                if not (isinstance(s, int) and s < 2):
                    pool.wait_ge(shifted, s - 1)
                nc.gpsimd.tensor_tensor(
                    max_rows[:, par].rearrange("p (b j) -> p b j", j=BLK),
                    neg_max[:, par].unsqueeze(2).to_broadcast([P, NBLK, BLK]),
                    id32b[:].unsqueeze(1).to_broadcast([P, NBLK, BLK]), ALU.mult).then_inc(max_spread, 1)

            def spread_inv(s, par):
                pool.wait_ge(inv_found, 2 * (s + 1))
                if not (isinstance(s, int) and s < 2):
                    pool.wait_ge(inv_ready, 2 * (s - 1))
                nc.gpsimd.tensor_tensor(
                    inv_rows[:, par].rearrange("p (b j) -> p b j", j=BLK),
                    inv[:, par].unsqueeze(2).to_broadcast([P, NBLK, BLK]),
                    id32f[:].unsqueeze(1).to_broadcast([P, NBLK, BLK]), ALU.mult).then_inc(inv_spread, 1)

            def residual(g, par):
                pool.wait_ge(xl_done, TPG * (g + 1))
                nc.gpsimd.tensor_tensor(rows[:, par, :, D:2 * D], x2[:], xl[:], ALU.add).then_inc(base_done, 1)
                nc.gpsimd.tensor_copy(rows[:, par, :, ID_AT:ID_AT + 1].bitcast(U32),
                                      token_f[:].unsqueeze(2)).then_inc(base_done, 1)
                pool.wait_ge(base_done, 3 * g + 2)
                settle_p(0)
                nc.gpsimd.tensor_scalar(token_f[:], token_f[:], float(GT), None, ALU.add).then_inc(base_done, 1)

            def scatter(g, par):
                pool.wait_ge(place_done, g + 1)
                pool.wait_ge(xn_done, TPG * (g + 1))
                pool.wait_ge(base_done, 3 * (g + 1))
                settle_p(1)
                for t in range(TPG):
                    pool.indirect_dma_start(
                        out=table[:, :], out_offset=bass.IndirectOffsetOnAxis(ap=place_u[:, par, t:t + 1], axis=0),
                        in_=rows[:, par, t, :], in_offset=None).then_inc(scattered, 16)

            def group(g, par, has_prev, has_next):
                for t in range(TPG):
                    s = TPG * g + t
                    if t == 0 and has_next:
                        root_x(g + 1)
                    if t == 2 and has_prev:
                        root_x2(g - 1)
                    if t >= 1 or has_prev:
                        spread_inv(s - 1, (t + 1) % 2)
                    spread_max(s, t % 2)
                    if t == 2 and has_prev:
                        residual(g - 1, 1 - par)
                    if t == 3 and has_prev:
                        scatter(g - 1, 1 - par)

            root_x(0)
            groups(pool, group)
            spread_inv(TILES - 1, 1)
            last = GROUPS - 1
            root_x2(last)
            residual(last, last % 2)
            scatter(last, last % 2)

            pool.wait_ge(pads_found, 1)
            for e in range(EXPERTS):
                pool.indirect_dma_start(
                    out=table[:, :], out_offset=bass.IndirectOffsetOnAxis(ap=pad_u[:, e:e + 1], axis=0),
                    in_=pad_row[:], in_offset=None).then_inc(padded, 16)

            def pair(j, k, turn, static):
                for n in range(2):
                    pool.wait_ge(fout_done, j + n + 1)
                    if static or n:
                        pool.wait_ge(settled, j + n)
                    settle_p(2).then_inc(settled, 1)
                    pool.indirect_dma_start(
                        out=out, out_offset=bass.IndirectOffsetOnAxis(
                            ap=frow[:, k + n, ID_AT:ID_AT + 1].bitcast(U32), axis=0),
                        in_=fout[:, k + n, :], in_offset=None, bounds_check=TOKENS - 1,
                        oob_is_err=False).then_inc(stored[k + n], 16)

            ffn_pairs(pool, pair)
            for k in range(FB):
                pool.wait_ge(stored[k], 16 * (FT // FB))

        @block.tensor
        def _(pe):
            mm = nc.tensor.matmul

            pe.wait_ge(weights_in, 64)
            for n, (left, right) in enumerate(((wqT, wkT), (wvT, wo_sb))):
                for q in range(HEADS // 4):
                    for h in (4 * q, 4 * q + 2, 4 * q + 1, 4 * q + 3):
                        r = HD * (h % 2)
                        b = banks[4 * n + 2 * (q % 2) + h % 2]
                        if h == 4 * q and q >= 2:
                            pe.wait_ge(m_copied if n else a_rest, 2 * (q - 1))
                        at = ((h // 2) % 2) * D
                        last = mm(b[:, at:at + D], left[r:r + HD, h // 2, :], right[r:r + HD, h // 2, :],
                                  start=True, stop=True, skip_group_check=True)
                    last.then_inc(fold_ready, 1)
            pe.wait_ge(consts_cast, 4)
            pe.wait_ge(a_rest, 8)
            pe.wait_ge(m_copied, 8)
            mm(MISC[:, 0:EXPERTS], ones_f[:], cent_sq[:], start=True, stop=True).then_inc(norm_ready, 1)

            def turn_x(g):
                pe.wait_ge(ln1_done, TPG * (g + 1))
                for t in range(TPG):
                    last = nc.tensor.transpose(MISC[:, t * P:(t + 1) * P], xln[:, t, :], ident[:])
                last.then_inc(xT_ready, 1)

            def queries(g, h, par):
                for n, (a, b) in enumerate(((a_hi, xT_hi), (a_lo, xT_hi), (a_hi, xT_lo))):
                    last = mm(g_bank(h)[:, :], a[:, h, :], b[:], start=(n == 0), stop=(n == 2))
                last.then_inc(g_ready, 1)

            def scores(s, t, par):
                for half in range(2):
                    for b in range(2):
                        last = mm(S_BANK[t % 2][half][b * SEQ:(b + 1) * SEQ, :],
                                  ctxT[:, par, t * P + b * SEQ:t * P + (b + 1) * SEQ],
                                  gq[:, par, 8 * half:8 * half + 8, t * P + b * SEQ:t * P + (b + 1) * SEQ],
                                  start=True, stop=True, skip_group_check=True)
                last.then_inc(scores_ready, 1)

            def shift(s, b):
                pe.wait_ge(max_spread, s + 1)
                for half in range(2):
                    last = mm(S_BANK[b][half][:, :], blk_b[:], max_rows[:, b, half * HALF:(half + 1) * HALF],
                              start=False, stop=True, skip_group_check=True)
                last.then_inc(shifted, 1)

            def spread(s, b, half):
                if half == 0:
                    pe.wait_ge(inv_spread, s + 1)
                else:
                    pe.wait_ge(probs_ready, 2 * s + 1)
                mm(R_BANK[:, :], blk_r[:], inv_rows[:, b, half * HALF:(half + 1) * HALF],
                   start=True, stop=True).then_inc(inv_ready, 1)

            def values(s, t, par, b2, n):
                half, b = n // 2, n % 2
                if b == 0:
                    pe.wait_ge(probs_ready, 2 * s + half + 1)
                if n:
                    pe.wait_ge(u_out, 4 * s + n)
                mm(U_BANK[:, :], ctxN[b * SEQ:(b + 1) * SEQ, par, t, :],
                   probs[b * SEQ:(b + 1) * SEQ, b2, half * HALF:(half + 1) * HALF],
                   start=True, stop=True).then_inc(u_ready, 1)

            def project(s, b2, half):
                pe.wait_ge(u_out, 4 * s + 2 * (half + 1))
                for h in range(HEADS // 2 * half, HEADS // 2 * (half + 1)):
                    last = mm(Y_BANK[:, 0:D], ut[:, b2, h, :], m_sb[:, h, :], start=(h == 0), stop=(h == HEADS - 1))
                if half:
                    last.then_inc(y_ready, 1)

            def turn_normed(g, par):
                pe.wait_ge(xn_done, TPG * (g + 1))
                for t in range(TPG):
                    last = nc.tensor.transpose(MISC[:, t * P:(t + 1) * P], rows[:, par, t, 0:D], ident[:])
                last.then_inc(xnT_ready, 1)

            def dots(g):
                pe.wait_ge(xnT_out, g + 1)
                for t in range(TPG):
                    last = mm(MISC[:, t * EXPERTS:(t + 1) * EXPERTS], xnT[:, t * P:(t + 1) * P], centT[:],
                              start=True, stop=True)
                last.then_inc(dots_ready, 1)

            def ranks(g):
                pe.wait_ge(onehot_done, g + 1)
                n = TPG * EXPERTS
                mm(MISC[:, 0:n], before_b[:], onehot[:].rearrange("p t e -> p (t e)"), start=True, stop=False)
                mm(MISC[:, 0:n], ones_b[:], earlier[:].rearrange("p t e -> p (t e)"),
                   start=False, stop=True).then_inc(ranks_ready, 1)

            pe.wait_ge(norm_taken, 1)
            turn_x(0)
            pe.wait_ge(a_split, HEADS // 2)
            pe.wait_ge(xT_hi_out, 1)
            pe.wait_ge(xT_lo_out, 1)
            for h in range(HEADS):
                before = [k for k in range(h) if g_bank(k) is g_bank(h)]
                if before:
                    pe.wait_ge(g_out, before[-1] + 1)
                queries(0, h, 0)
            pe.wait_ge(ctxT_in, 16)
            pe.wait_ge(ctxN_in, 16)

            def heads_at(g, par, has_prev, t, place):
                for h in HEADS_AT[t][place]:
                    bank = g_bank(h)
                    if t == 1 and h == 0:
                        pe.wait_ge(xT_hi_out, g + 2)
                        pe.wait_ge(xT_lo_out, g + 2)
                    before = [k for k in range(h) if g_bank(k) is bank]
                    if bank is Y_BANK and not any(k in sum(HEADS_AT[t], []) for k in before):
                        if t == 3 or has_prev:
                            pe.wait_ge(x2_done, TPG * g + t - 2)
                    if t == 3 and bank is MISC and h == HEADS_AT[t][0][0] and has_prev:
                        pe.wait_ge(dots_taken, g)
                    elif before:
                        pe.wait_ge(g_out, HEADS * (g + 1) + before[-1] + 1)
                    queries(g + 1, h, 1 - par)

            def last_in(bank, t):
                return max(h for h in sum(HEADS_AT[t], []) if g_bank(h) is bank)

            def group(g, par, has_prev, has_next):
                for t in range(TPG):
                    s = TPG * g + t
                    if t == 0:
                        pe.wait_ge(g_out, HEADS * (g + 1))
                        pe.wait_ge(ctxT_in, 16 * (g + 1))
                    if t == 3 and has_prev:
                        dots(g - 1)
                    if t >= 2 or has_prev:
                        pe.wait_ge(exp_done, 2 * (s - 1))
                    scores(s, t, par)
                    tv, pv = (t - 2, par) if t >= 2 else (t + 2, 1 - par)
                    if t >= 2 or has_prev:
                        spread(s - 2, t % 2, 0)
                    if has_next:
                        heads_at(g, par, has_prev, t, 0)
                    if t >= 1 or has_prev:
                        shift(s - 1, (t + 1) % 2)
                    if t >= 2 or has_prev:
                        spread(s - 2, t % 2, 1)
                        if t == 2:
                            pe.wait_ge(ctxN_in, 16 * (g + 1))
                        values(s - 2, tv, pv, t % 2, 0)
                    if has_next:
                        heads_at(g, par, has_prev, t, 1)
                    if t >= 2 or has_prev:
                        values(s - 2, tv, pv, t % 2, 1)
                    if has_next:
                        heads_at(g, par, has_prev, t, 2)
                    if t >= 2 or has_prev:
                        values(s - 2, tv, pv, t % 2, 2)
                        if has_next and HEADS_AT[t][0]:
                            pe.wait_ge(g_out, HEADS * (g + 1) + last_in(Y_BANK, t) + 1)
                        elif not (isinstance(g, int) and s <= 2):
                            pe.wait_ge(x2_done, s - 2)
                        project(s - 2, t % 2, 0)
                        values(s - 2, tv, pv, t % 2, 3)
                    if has_next:
                        heads_at(g, par, has_prev, t, 3)
                    if t == 0 and has_next:
                        turn_x(g + 1)
                    if t >= 2 or has_prev:
                        project(s - 2, t % 2, 1)
                    if t == 2 and has_prev:
                        if has_next:
                            pe.wait_ge(g_out, HEADS * (g + 1) + last_in(MISC, t) + 1)
                        turn_normed(g - 1, 1 - par)
                    if t == 3 and has_prev:
                        if has_next:
                            pe.wait_ge(g_out, HEADS * (g + 1) + last_in(MISC, t) + 1)
                        else:
                            pe.wait_ge(dots_taken, g)
                        ranks(g - 1)

            groups(pe, group)
            last = GROUPS - 1
            for s in (TILES, TILES + 1):
                spread(s - 2, s % 2, 0)
                if s == TILES:
                    shift(s - 1, 1)
                spread(s - 2, s % 2, 1)
                for n in range(3):
                    values(s - 2, TPG + s - 2 - TILES, last % 2, s % 2, n)
                pe.wait_ge(x2_done, s - 2)
                project(s - 2, s % 2, 0)
                values(s - 2, TPG + s - 2 - TILES, last % 2, s % 2, 3)
                project(s - 2, s % 2, 1)
            pe.wait_ge(ranks_taken, last)
            turn_normed(last, last % 2)
            dots(last)
            pe.wait_ge(dots_taken, last + 1)
            ranks(last)
            pe.wait_ge(ranks_taken, last + 1)
            mm(MISC[:, 0:EXPERTS], ones_b[:], seen[:], start=True, stop=True).then_inc(counts_ready, 1)

            pe.wait_ge(tiles_found, 1)
            pe.wait_ge(ffn_in, 32)

            def pair(j, k, turn, static):
                for n in range(2):
                    pe.wait_ge(frow_in[k + n], 16 * (turn + 1))
                    last = nc.tensor.transpose(TURN_BANK[:, n * P:(n + 1) * P], frow[:, k + n, 0:D], ident[:])
                last.then_inc(fxT_ready, 1)
                e = [pe.value_load(t_expert[0:1, bass.ds(j + n, 1)], min_val=0, max_val=EXPERTS - 1)
                     for n in range(2)]
                pe.wait_ge(fxT_out, FB // 2 * turn + k // 2 + 1)
                for n in range(2):
                    mm(UP_BANK[n][:, :], fxT[:, n * P:(n + 1) * P], upw[:, bass.ds(e[n] * (2 * HID), 2 * HID)],
                       start=True, stop=True).then_inc(up_ready, 1)
                for n in range(2):
                    pe.wait_ge(act_done, j + n + 1)
                    for c in range(2):
                        last = nc.tensor.transpose(ACT_BANK[n][:, c * P:(c + 1) * P], act[:, n, c * P:(c + 1) * P],
                                                   ident[:])
                    last.then_inc(actT_ready, 1)
                for n in range(2):
                    pe.wait_ge(actT_out, j + n + 1)
                    if static >= 2:
                        pe.wait_ge(fout_done, j + n - 1)
                    for c in range(2):
                        last = mm(DOWN_BANK[n][:, 0:D], actT[:, n, c * P:(c + 1) * P],
                                  downw[:, bass.ds(e[n] * (2 * D) + c * D, D)], start=(c == 0), stop=(c == 1))
                    last.then_inc(down_ready, 1)

            ffn_pairs(pe, pair)

        @block.scalar
        def _(sc):
            copy = nc.scalar.copy

            for n in range(2):
                for q in range(HEADS // 4):
                    sc.wait_ge(fold_ready, 4 * n + q + 1)
                    for r in range(2):
                        b = banks[4 * n + 2 * (q % 2) + r]
                        src = b[:, 0:2 * D].rearrange("p (k d) -> p k d", k=2)
                        if n == 0:
                            copy(a_hi[:, 4 * q + r:4 * q + r + 3:2, :], src).then_inc(a_split, 1)
                        else:
                            copy(m_sb[:, 4 * q + r:4 * q + r + 3:2, :], src).then_inc(m_copied, 1)

            def turned_x(g):
                sc.wait_ge(xT_ready, g + 1)
                copy(xT_hi[:], MISC[:]).then_inc(xT_hi_out, 1)

            def queries_out(g, h, par):
                sc.wait_ge(g_ready, HEADS * g + h + 1)
                copy(gq[:, par, h, :], g_bank(h)[:]).then_inc(g_out, 1)

            def exps(s, b):
                sc.wait_ge(shifted, s + 1)
                for half in range(2):
                    nc.scalar.activation(probs[:, b, half * HALF:(half + 1) * HALF], S_BANK[b][half][:],
                                         ACT.Exp, scale=SCORE_SCALE).then_inc(exp_done, 1)

            def values_out(s, b2, n):
                half, b = n // 2, n % 2
                if n == 0 and not (isinstance(s, int) and s < 2):
                    sc.wait_ge(y_ready, s - 1)
                sc.wait_ge(u_ready, 4 * s + n + 1)
                copy(ut[:, b2, 8 * half:8 * half + 8, b * SEQ:(b + 1) * SEQ],
                     U_BANK[:].rearrange("p (h q) -> p h q", q=SEQ)).then_inc(u_out, 1)

            def normed_out(g):
                sc.wait_ge(xnT_ready, g + 1)
                copy(xnT[:], MISC[:]).then_inc(xnT_out, 1)

            turned_x(0)
            for h in range(HEADS):
                queries_out(0, h, 0)

            def group(g, par, has_prev, has_next):
                for t in range(TPG):
                    s = TPG * g + t
                    valued = t >= 2 or has_prev

                    def heads(place):
                        for h in HEADS_AT[t][place] if has_next else []:
                            queries_out(g + 1, h, 1 - par)

                    heads(0)
                    if t >= 1 or has_prev:
                        exps(s - 1, (t + 1) % 2)
                    if valued:
                        values_out(s - 2, t % 2, 0)
                    heads(1)
                    if valued:
                        values_out(s - 2, t % 2, 1)
                    heads(2)
                    if valued:
                        values_out(s - 2, t % 2, 2)
                        values_out(s - 2, t % 2, 3)
                    heads(3)
                    if t == 0 and has_next:
                        turned_x(g + 1)
                    if t == 2 and has_prev:
                        normed_out(g - 1)

            groups(sc, group)
            exps(TILES - 1, 1)
            for s in (TILES - 2, TILES - 1):
                for n in range(4):
                    values_out(s, s % 2, n)
            normed_out(GROUPS - 1)

            def pair(j, k, turn, static):
                sc.wait_ge(fxT_ready, FB // 2 * turn + k // 2 + 1)
                copy(fxT[:], TURN_BANK[:, 0:2 * P]).then_inc(fxT_out, 1)
                for n in range(2):
                    sc.wait_ge(up_ready, j + n + 1)
                    nc.scalar.activation(gate[:, n, :], UP_BANK[n][:, HID:2 * HID], ACT.Silu).then_inc(gated, 1)
                for n in range(2):
                    sc.wait_ge(actT_ready, j + n + 1)
                    copy(actT[:, n, :], ACT_BANK[n][:, 0:HID]).then_inc(actT_out, 1)

            ffn_pairs(sc, pair)

        @block.vector
        def _(dve):
            v = nc.vector
            seq = Chain(dve, dve_seq)

            dve.wait_ge(small_in, 32)
            v.tensor_tensor(cent_sq[:], centT[:], centT[:], ALU.mult).then_inc(consts_cast, 1)
            dve.wait_ge(consts_made, 2)
            seq.mark(v.tensor_copy(id32b[:], id32f[:]))
            seq.mark(v.tensor_copy(blk_b[:], blk_f[:]))
            seq.mark(v.tensor_copy(blk_r[:], blk_f[:]))
            seq.mark(v.tensor_copy(ones_b[:], ones_f[:]))
            seq.wait()
            v.memset(key_max2[:], 0.0).then_inc(consts_cast, 1)
            v.memset(key_sum2[:], 0.0).then_inc(consts_cast, 1)
            v.memset(square[:], 0.0).then_inc(consts_cast, 1)

            def statistics(src, stats, mv):
                for t in range(TPG):
                    seq.mark(v.bn_stats(stats[:, t, :], src[:, t, :]))
                seq.wait()
                settle_v()
                for t in range(TPG):
                    seq.mark(v.bn_aggr(mv[:, t, :], stats[:, t, :]))
                seq.wait()

            def measure_x(g):
                dve.wait_ge(x_in, 16 * (g + 1))
                statistics(xin, stats1, mv1)
                v.tensor_scalar(var1[:], mv1[:, :, 1], LN_EPS, None, ALU.add).then_inc(var1_done, 1)

            def norm_x(g):
                dve.wait_ge(rstd1_done, g + 1)
                if not (isinstance(g, int) and g == 0):
                    dve.wait_ge(xT_ready, g)
                for t in range(TPG):
                    v.tensor_scalar(xln[:, t, :], xin[:, t, :], mv1[:, t, 0:1], rstd1[:, t:t + 1],
                                    ALU.subtract, ALU.mult).then_inc(ln1_done, 1)

            def split_x(g):
                dve.wait_ge(xT_hi_out, g + 1)
                v.tensor_tensor(xT_lo[:], MISC[:], xT_hi[:].bitcast(F32), ALU.subtract).then_inc(xT_lo_out, 1)

            def across_halves(dst, src):
                for q in range(P // BLK):
                    seq.mark(v.tensor_copy(dst[q * BLK:(q + 1) * BLK, :], src[(q ^ 1) * BLK:((q ^ 1) + 1) * BLK, :]))
                seq.wait()

            def maxima(s, b):
                dve.wait_ge(scores_ready, s + 1)
                for half in range(2):
                    seq.mark(v.transpose(turned[:, half * HALF:(half + 1) * HALF], S_BANK[b][half][:]))
                seq.wait()
                seq.then(v.tensor_reduce(key_max[:], turned[:].rearrange("p (b k) -> p b k", k=BLK), AX_X, ALU.max))
                across_halves(key_max2, key_max)
                seq.then(v.tensor_tensor(top[:], key_max[:], key_max2[:], ALU.max))
                if not (isinstance(s, int) and s < 2):
                    dve.wait_ge(max_spread, s - 1)
                v.tensor_scalar(neg_max[:, b], top[:], -1.0, None, ALU.mult).then_inc(max_found, 1)
                dve.wait_ge(max_found, 3 * s + 1)
                for q in (1, 3):
                    r = slice(q * BLK, (q + 1) * BLK)
                    v.scalar_tensor_tensor(out=neg_max[r, b], in0=top[r, :], scalar=-1.0, in1=neg_max[r, b],
                                           op0=ALU.mult, op1=ALU.subtract).then_inc(max_found, 1)

            def sums(s, b):
                for half in range(2):
                    dve.wait_ge(exp_done, 2 * s + half + 1)
                    r = slice(half * HALF, (half + 1) * HALF)
                    seq.mark(v.transpose(turned_p[:, r], probs[:, b, r]))
                seq.wait()
                seq.then(v.tensor_reduce(key_sum[:], turned_p[:].rearrange("p (b k) -> p b k", k=BLK), AX_X, ALU.add))
                across_halves(key_sum2, key_sum)
                seq.then(v.tensor_tensor(total[:], key_sum[:], key_sum2[:], ALU.add))
                if not (isinstance(s, int) and s < 2):
                    dve.wait_ge(inv_spread, s - 1)
                seq.then(v.reciprocal(inv[:, b], total[:]))
                seq.then(v.tensor_copy(inv_hi[:], inv[:, b]))
                for q in (1, 3):
                    r = slice(q * BLK, (q + 1) * BLK)
                    v.tensor_tensor(inv[r, b], inv[r, b], inv_hi[r, :].bitcast(F32),
                                    ALU.subtract).then_inc(inv_found, 1)

            def normalise(s, b):
                for half in range(2):
                    dve.wait_ge(inv_ready, 2 * s + half + 1)
                    r = slice(half * HALF, (half + 1) * HALF)
                    v.tensor_tensor(probs[:, b, r], probs[:, b, r], R_BANK[:],
                                    ALU.mult).then_inc(probs_ready, 1)

            def add_residual(s, g, t, par):
                dve.wait_ge(y_ready, s + 1)
                if t == 0:
                    if not (isinstance(s, int) and s == 0):
                        dve.wait_ge(base_done, 3 * g)
                    dve.wait_ge(xres_in, 16 * (g + 1))
                v.tensor_tensor(x2[:, t, :], Y_BANK[:, 0:D], xres[:, par, t, :], ALU.add).then_inc(x2_done, 1)

            def measure_x2(g):
                dve.wait_ge(x2_done, TPG * (g + 1))
                statistics(x2, stats2, mv2)
                var = mv2[:, :, 1]
                seq.then(v.tensor_scalar(spread2[:, 0, :], var, LN_EPS, None, ALU.add))
                seq.then(v.reciprocal(var_inv[:], spread2[:, 0, :]))
                seq.then(v.tensor_tensor(var_inv[:], var, var_inv[:], ALU.mult))
                v.tensor_scalar(spread2[:, 1, :], var_inv[:], RMS_EPS, None, ALU.add).then_inc(spread2_done, 1)

            def norm_x2(g, par):
                dve.wait_ge(root2_done, g + 1)
                for t in range(TPG):
                    v.tensor_scalar(xl[:, t, :], x2[:, t, :], mv2[:, t, 0:1], root2[:, 0, t:t + 1],
                                    ALU.subtract, ALU.mult).then_inc(xl_done, 1)
                dve.wait_ge(xl_done, TPG * (g + 1))
                dve.wait_ge(scattered, 16 * (TPG * g + 1))
                for t in range(TPG):
                    v.scalar_tensor_tensor(out=rows[:, par, t, 0:D], in0=xl[:, t, :], scalar=root2[:, 1, t:t + 1],
                                           in1=scale_b[:], op0=ALU.mult, op1=ALU.mult).then_inc(xn_done, 1)
                dve.wait_ge(xn_done, TPG * (g + 1))
                for t in range(TPG):
                    seq.mark(v.tensor_tensor_reduce(square[:, t, :], rows[:, par, t, 0:D], rows[:, par, t, 0:D], 1.0, 0.0,
                                                    ALU.mult, ALU.add, norm2[:, t:t + 1]))
                seq.wait()
                seq.then(v.tensor_tensor(norms[:], norm2[:].unsqueeze(2).to_broadcast([P, TPG, EXPERTS]),
                                         cent_norm[:].unsqueeze(1).to_broadcast([P, TPG, EXPERTS]), ALU.add))

            def take_dots(g):
                dve.wait_ge(dots_ready, g + 1)
                v.scalar_tensor_tensor(out=dist[:].rearrange("p t e -> p (t e)"), in0=MISC[:, 0:TPG * EXPERTS],
                                       scalar=-2.0, in1=norms[:].rearrange("p t e -> p (t e)"), op0=ALU.mult,
                                       op1=ALU.add).then_inc(dots_taken, 1)

            def choose(g):
                def experts(ap):
                    return ap.unsqueeze(1).to_broadcast([P, TPG, EXPERTS])

                dve.wait_ge(dots_taken, g + 1)
                seq.then(v.tensor_reduce(least[:], dist[:], AX_X, ALU.min))
                seq.then(v.tensor_tensor(cand[:], dist[:], least[:].unsqueeze(2).to_broadcast([P, TPG, EXPERTS]),
                                         ALU.is_le))
                seq.then(v.tensor_tensor(cand[:], cand[:], experts(expert_m8[:]), ALU.mult))
                seq.then(v.tensor_reduce(chosen[:], cand[:], AX_X, ALU.min))
                seq.then(v.tensor_tensor(onehot[:], experts(expert_m8[:]),
                                         chosen[:].unsqueeze(2).to_broadcast([P, TPG, EXPERTS]), ALU.is_equal))
                seq.then(v.tensor_copy(earlier[:, 0, :], seen[:]))
                for t in range(1, TPG):
                    seq.then(v.tensor_tensor(earlier[:, t, :], earlier[:, t - 1, :], onehot[:, t - 1, :], ALU.add))
                v.tensor_tensor(seen[:], earlier[:, TPG - 1, :], onehot[:, TPG - 1, :],
                                ALU.add).then_inc(onehot_done, 1)

            def places(g, par):
                dve.wait_ge(ranks_ready, g + 1)
                v.tensor_tensor(place[:], MISC[:, 0:TPG * EXPERTS].rearrange("p (t e) -> p t e", e=EXPERTS),
                                region_of[:].unsqueeze(1).to_broadcast([P, TPG, EXPERTS]),
                                ALU.add).then_inc(ranks_taken, 1)
                dve.wait_ge(ranks_taken, g + 1)
                seq.then(v.tensor_tensor(place[:], place[:], onehot[:], ALU.mult))
                seq.then(v.tensor_reduce(place_f[:], place[:], AX_X, ALU.add))
                v.tensor_copy(place_u[:, par, :], place_f[:]).then_inc(place_done, 1)

            for q in range(HEADS // 4):
                dve.wait_ge(a_split, 2 * q + 2)
                for r in range(2):
                    b = banks[2 * (q % 2) + r]
                    v.tensor_tensor(a_lo[:, 4 * q + r:4 * q + r + 3:2, :],
                                    b[:, 0:2 * D].rearrange("p (k d) -> p k d", k=2),
                                    a_hi[:, 4 * q + r:4 * q + r + 3:2, :].bitcast(F32),
                                    ALU.subtract).then_inc(a_rest, 1)
            measure_x(0)
            norm_x(0)
            dve.wait_ge(norm_ready, 1)
            v.tensor_copy(cent_norm[:], MISC[:, 0:EXPERTS]).then_inc(norm_taken, 1)
            split_x(0)

            def group(g, par, has_prev, has_next):
                for t in range(TPG):
                    s = TPG * g + t
                    if t == 3:
                        add_residual(s - 3, g, 0, par)
                    elif has_prev:
                        add_residual(s - 3, g - 1, t + 1, 1 - par)
                    if t == 1 and has_next:
                        split_x(g + 1)
                    if t == 3 and has_prev:
                        take_dots(g - 1)
                    if t >= 2 or has_prev:
                        normalise(s - 2, t % 2)
                    if t == 0 and has_next:
                        measure_x(g + 1)
                    if t == 2 and has_prev:
                        measure_x2(g - 1)
                    if t == 3 and has_prev:
                        choose(g - 1)
                    if t >= 1 or has_prev:
                        sums(s - 1, (t + 1) % 2)
                    if t == 0 and has_next:
                        norm_x(g + 1)
                    if t == 2 and has_prev:
                        norm_x2(g - 1, 1 - par)
                    maxima(s, t % 2)
                    if t == 3 and has_prev:
                        places(g - 1, 1 - par)

            group(0, 0, False, True)
            with dve.Fori(0, LOOPS) as i:
                seq.loop(i, DVE_PER_TURN)
                for k in range(2):
                    group(1 + k + 2 * i, (1 + k) % 2, True, True)
                seq.end_loop(LOOPS)
            last = GROUPS - 1
            group(last, last % 2, True, False)
            add_residual(TILES - 3, last, 1, last % 2)
            normalise(TILES - 2, 0)
            sums(TILES - 1, 1)
            add_residual(TILES - 2, last, 2, last % 2)
            normalise(TILES - 1, 1)
            add_residual(TILES - 1, last, 3, last % 2)
            measure_x2(last)
            norm_x2(last, last % 2)
            take_dots(last)
            choose(last)
            places(last, last % 2)

            dve.wait_ge(counts_ready, 1)
            seq.then(v.tensor_copy(count[:], MISC[:, 0:EXPERTS]))
            seq.mark(v.tensor_tensor(pad_at[:], count[:], region_of[:], ALU.add))
            seq.then(v.tensor_scalar(count_i[:], count[:], float(P - 1), None, ALU.add))
            seq.mark(v.tensor_scalar(count_i[:], count_i[:], P.bit_length() - 1, None, ALU.logical_shift_right))
            seq.wait()
            v.tensor_scalar(pad_u[:], pad_at[:], part_f[:, 0:1], None, ALU.add).then_inc(pads_found, 1)
            seq.then(v.tensor_copy(ntile[:], count_i[:]))
            seq.then(v.tensor_tensor(upto[:], upto[:], ntile[:].unsqueeze(1).to_broadcast([P, EXPERTS, EXPERTS]),
                                     ALU.mult))
            seq.then(v.tensor_reduce(cumul[:], upto[:], AX_X, ALU.add))
            seq.then(v.tensor_tensor(done[:], tile_no[:].unsqueeze(2).to_broadcast([P, FT, EXPERTS]),
                                     cumul[:].unsqueeze(1).to_broadcast([P, FT, EXPERTS]), ALU.is_ge))
            seq.mark(v.tensor_reduce(tile_e[:], done[:], AX_X, ALU.add))
            seq.then(v.tensor_tensor(done_n[:], done[:], ntile[:].unsqueeze(1).to_broadcast([P, FT, EXPERTS]),
                                     ALU.mult))
            seq.then(v.tensor_reduce(tile_b[:], done_n[:], AX_X, ALU.add))
            seq.then(v.tensor_tensor(tile_b[:], tile_no[:], tile_b[:], ALU.subtract))
            seq.mark(v.tensor_scalar(tile_r[:], tile_e[:], float(REGION), None, ALU.mult))
            seq.then(v.tensor_scalar(tile_e[:], tile_e[:], float(EXPERTS - 1), None, ALU.min))
            seq.then(v.scalar_tensor_tensor(out=tile_r[:], in0=tile_b[:], scalar=float(P), in1=tile_r[:],
                                            op0=ALU.mult, op1=ALU.add))
            seq.mark(v.tensor_copy(t_expert[:], tile_e[:]))
            seq.then(v.tensor_copy(t_row[:], tile_r[:]))
            v.memset(spare_v[:], 0.0).then_inc(tiles_found, 1)

            def pair(j, k, turn, static):
                for n in range(2):
                    dve.wait_ge(gated, j + n + 1)
                    v.tensor_tensor(act[:, n, :], gate[:, n, :], UP_BANK[n][:, 0:HID], ALU.mult).then_inc(act_done, 1)
                for n in range(2):
                    dve.wait_ge(down_ready, j + n + 1)
                    v.tensor_tensor(fout[:, k + n, :], DOWN_BANK[n][:, 0:D], frow[:, k + n, D:2 * D],
                                    ALU.add).then_inc(fout_done, 1)

            ffn_pairs(dve, pair)


DVE_PER_TURN = 214


def kernel(x, ctx_1024, L0_xattn_Wq, L0_xattn_Wk, L0_xattn_Wv, L0_xattn_Wo, L0_ffn_scale, L0_ffn_centroids,
           L0_ffn_up_w, L0_ffn_down_w):
    import numpy as np
    from concourse import bacc
    from concourse.bass_utils import run_bass_kernel_spmd

    def lay(a):
        return np.ascontiguousarray(a)

    flat = np.asarray(ctx_1024).reshape(TOKENS, D)
    arrays = {
        "x": lay(np.asarray(x).reshape(TOKENS, D)),
        "ctx": lay(flat),
        "ctx_t": lay(flat.T),
        "wq_t": lay(np.asarray(L0_xattn_Wq).T),
        "wk_t": lay(np.asarray(L0_xattn_Wk).T),
        "wv_t": lay(np.asarray(L0_xattn_Wv).T),
        "wo": lay(L0_xattn_Wo),
        "scale": lay(np.asarray(L0_ffn_scale).reshape(1, D)),
        "cent_t": lay(np.asarray(L0_ffn_centroids).T),
        "up_w": lay(L0_ffn_up_w),
        "down_w": lay(L0_ffn_down_w),
    }
    nc = bacc.Bacc("TRN2", target_bir_lowering=False, num_devices=1)
    args = [nc.dram_tensor(n, a.shape, mybir.dt.from_np(a.dtype), kind="ExternalInput").ap()
            for n, a in arrays.items()]
    out = nc.dram_tensor("out", (TOKENS, D), F32, kind="ExternalOutput").ap()
    xattn_ffn(nc, *args, out)
    r = run_bass_kernel_spmd(nc, [arrays], core_ids=[0])
    return r.results[0]["out"].reshape(TOKENS // SEQ, SEQ, D)
```

```python
from contextlib import ExitStack

import concourse.bass as bass
from concourse import mybir

F32 = mybir.dt.float32
F32R = mybir.dt.float32r
BF16 = mybir.dt.bfloat16
U32 = mybir.dt.uint32
I32 = mybir.dt.int32
ALU = mybir.AluOpType
ACT = mybir.ActivationFunctionType
AX_X = mybir.AxisListType.X

P = 128
D = 128
SEQ = 64
TOKENS = 4096
HEADS = 16
HD = 64
TILES = TOKENS // P
TPG = 4
GROUPS = TILES // TPG
GT = TPG * P
HALF = HEADS // 2 * SEQ
BLK = 32
NBLK = HEADS * SEQ // BLK
SCORE_SCALE = HD ** -0.5
LN_EPS = 1e-5
RMS_EPS = 1e-6

EXPERTS = 8
HID = 256
ROW = 2 * D + 4
ID_AT = 2 * D
REGION = TOKENS + P
NO_TOKEN = 1 << 20
FB = 10
FT = -(-(TILES + EXPERTS - 1) // FB) * FB
LAG = 4
HEADS_PER_STEP = HEADS // TPG
LOOPS = (GROUPS - 2) // 2
UP_PIECES = 4
UP_PIECE = EXPERTS * 2 * HID // UP_PIECES


def xattn_ffn(nc, x, ctx, ctx_t, wq_t, wk_t, wv_t, wo, scale, cent_t, up_w, down_w, out):
    x_v = x.rearrange("(g t p) d -> g p t d", t=TPG, p=P)
    ctx_v = ctx.rearrange("(g t p) d -> g p t d", t=TPG, p=P)
    ctxt_v = ctx_t.rearrange("d (g n) -> g d n", g=GROUPS)
    table = nc.dram_tensor("sorted_rows", (EXPERTS * REGION + P, ROW), F32)

    with ExitStack() as es:
        def sb(name, shape, dt=F32):
            return es.enter_context(nc.sbuf_tensor(name, shape, dt))

        def sem(name):
            return es.enter_context(nc.semaphore(name))

        banks = [es.enter_context(nc.psum_tensor(f"bank{i}", [P, 512], F32)) for i in range(8)]
        S_BANK = [banks[0:2], banks[2:4]]
        Y_BANK, MISC = banks[4], banks[5]
        U_BANK, R_BANK = banks[6], banks[7]
        VALUES_BANK = (U_BANK, R_BANK)
        FOLD_BANKS = (banks[0:2], banks[2:4], banks[6:8])
        TURN_BANK, UP_BANK, ACT_BANK, DOWN_BANK = banks[0], banks[2:4], banks[4:6], banks[6:8]

        parts = sb("parts", [P, 2, HEADS, D], F32R)
        a_hi, a_lo = parts[:, 0], parts[:, 1]
        m_sb = sb("m_sb", [P, HEADS, D])
        upw = sb("upw", [P, EXPERTS * 2 * HID])
        downw = sb("downw", [P, EXPERTS * 2 * D])
        scale_b = sb("scale_b", [P, D])
        centT = sb("centT", [P, EXPERTS])
        cent_sq = sb("cent_sq", [P, EXPERTS])
        cent_norm = sb("cent_norm", [P, EXPERTS])
        ident = sb("ident", [P, P])
        id32f = sb("id32f", [P, BLK])
        id32b = sb("id32b", [P, BLK], BF16)
        blk_f = sb("blk_f", [P, P])
        blk_b = sb("blk_b", [P, P], BF16)
        blk_r = sb("blk_r", [P, P], F32R)
        ones_f = sb("ones_f", [P, P])
        ones_b = sb("ones_b", [P, P], BF16)
        before_b = sb("before_b", [P, P], BF16)
        expert_m8 = sb("expert_m8", [P, EXPERTS])
        region_of = sb("region_of", [P, EXPERTS])

        xin = sb("xin", [P, TPG, D])
        xres = sb("xres", [P, 2, TPG, D])
        ctxT = sb("ctxT", [P, 2, GT])
        ctxN = sb("ctxN", [P, 2, TPG, D])
        stats1 = sb("stats1", [P, TPG, 6])
        mv1 = sb("mv1", [P, TPG, 2])
        var1 = sb("var1", [P, TPG])
        rstd1 = sb("rstd1", [P, TPG])
        xln = sb("xln", [P, TPG, D])
        rounded = sb("rounded", [P, 8, GT], F32R)
        xT_hi, xT_lo = rounded[:, 0:2], rounded[:, 2:4]
        inv_rows = rounded[:, 4:8].rearrange("p (b k) n -> p b (k n)", b=2)
        up_hi = parts[:].rearrange("p a h d -> p (a h d)")
        up_lo = rounded[:].rearrange("p a n -> p (a n)")
        gq = sb("gq", [P, 2, HEADS, GT])
        turned = sb("turned", [P, 2 * HALF])
        turned_p = sb("turned_p", [P, 2 * HALF])
        keys = sb("keys", [P, 2, NBLK])
        others = sb("others", [P, 2, NBLK])
        top = sb("top", [P, NBLK])
        neg_max = sb("neg_max", [P, 2, NBLK], BF16)
        max_rows = sb("max_rows", [P, 2, 2 * HALF], BF16)
        probs = sb("probs", [P, 2, 2 * HALF])
        total = sb("total", [P, NBLK])
        inv = sb("inv", [P, 2, NBLK])
        inv_hi = sb("inv_hi", [P, NBLK], F32R)
        ut = sb("ut", [P, 2, HEADS, P])
        weights = ut[:].rearrange("p a (b h) d -> p (a b) h d", b=2)
        wqT, wkT, wvT, wo_sb = (weights[:, n] for n in range(4))
        x2 = sb("x2", [P, TPG, D])
        stats2 = sb("stats2", [P, TPG, 6])
        mv2 = sb("mv2", [P, TPG, 2])
        spread2 = sb("spread2", [P, 2, TPG])
        var_inv = sb("var_inv", [P, TPG])
        root2 = sb("root2", [P, 2, TPG])
        power = sb("power", [P, 2 * TPG])
        xl = sb("xl", [P, TPG, D])
        square = sb("square", [P, TPG, D])
        norm2 = sb("norm2", [P, TPG])
        rows = sb("rows", [P, 2, TPG, ROW])
        xnT = sb("xnT", [P, GT])
        norms = sb("norms", [P, TPG, EXPERTS])
        dot = sb("dot", [P, TPG * EXPERTS])
        rank = sb("rank", [P, TPG * EXPERTS])
        dist = sb("dist", [P, TPG, EXPERTS])
        least = sb("least", [P, TPG])
        cand = sb("cand", [P, TPG, EXPERTS])
        chosen = sb("chosen", [P, TPG])
        onehot = sb("onehot", [P, TPG, EXPERTS], BF16)
        chose = sb("chose", [P, EXPERTS])
        seen = sb("seen", [P, EXPERTS], BF16)
        place = sb("place", [P, TPG, EXPERTS])
        place_f = sb("place_f", [P, TPG])
        place_u = sb("place_u", [P, 2, TPG], U32)
        token_f = sb("token_f", [P, TPG])

        count = sb("count", [P, EXPERTS])
        count_i = sb("count_i", [P, EXPERTS], I32)
        ntile = sb("ntile", [P, EXPERTS])
        upto = sb("upto", [P, EXPERTS, EXPERTS])
        cumul = sb("cumul", [P, EXPERTS])
        pad_at = sb("pad_at", [P, EXPERTS])
        pad_i = sb("pad_i", [P, EXPERTS], I32)
        part_f = sb("part_f", [P, 1])
        pad_row = sb("pad_row", [P, ROW])
        tile_no = sb("tile_no", [P, FT])
        tile_e = sb("tile_e", [P, FT])
        tile_b = sb("tile_b", [P, FT])
        tile_r = sb("tile_r", [P, FT])
        pair_e = sb("pair_e", [P, FT // 2 + 4])
        four_e = sb("four_e", [P, FT // 2 + 2])
        t_experts = sb("t_experts", [P, FT // 2 + 2], I32)
        t_row = sb("t_row", [P, FT], I32)

        spare_v = sb("spare_v", [P, 1])
        spare_p = sb("spare_p", [P, 3])
        spare_s = sb("spare_s", [P, 1])
        room = gq[:, 0].rearrange("p h n -> p (h n)")
        taken = [0]

        def from_queries(shape):
            n = shape[0] * shape[1]
            taken[0] += n
            return room[:, taken[0] - n:taken[0]].rearrange("p (a b) -> p a b", a=shape[0])

        frow = from_queries([FB, ROW])
        done = from_queries([FT, EXPERTS])
        done_n = from_queries([FT, EXPERTS])
        numbers = sb("numbers", [P, FB], U32)
        fxT_hi = sb("fxT_hi", [P, 2 * P], F32R)
        fxT_lo = sb("fxT_lo", [P, 2 * P], F32R)
        gate = from_queries([2, HID])
        act = from_queries([2, HID])
        actT = from_queries([2, HID])
        fout = from_queries([FB, D])

        qk_weights_in = sem("qk_weights_in")
        vo_weights_in = sem("vo_weights_in")
        ffn_in = sem("ffn_in")
        small_in = sem("small_in")
        x_in = sem("x_in")
        x1_in = sem("x1_in")
        xres_in = sem("xres_in")
        ctxT_in = sem("ctxT_in")
        ctxN_in = sem("ctxN_in")
        pool_seq = sem("pool_seq")
        consts_made = sem("consts_made")
        dve_seq = sem("dve_seq")
        consts_cast = sem("consts_cast")
        fold_ready = sem("fold_ready")
        a_rest = sem("a_rest")
        m_copied = sem("m_copied")
        a_split = sem("a_split")
        norm_squares = sem("norm_squares")
        norm_ready = sem("norm_ready")
        norm_taken = sem("norm_taken")
        var1_done = sem("var1_done")
        rstd1_done = sem("rstd1_done")
        spread2_done = sem("spread2_done")
        root2_done = sem("root2_done")
        ln1_done = sem("ln1_done")
        xT_ready = sem("xT_ready")
        xT_hi_out = sem("xT_hi_out")
        xT_lo_out = sem("xT_lo_out")
        g_ready = sem("g_ready")
        g_out = sem("g_out")
        scores_ready = sem("scores_ready")
        max_found = sem("max_found")
        max_spread = sem("max_spread")
        shifted = sem("shifted")
        exp_done = sem("exp_done")
        inv_found = sem("inv_found")
        inv_spread = sem("inv_spread")
        inv_ready = sem("inv_ready")
        probs_ready = sem("probs_ready")
        u_ready = sem("u_ready")
        u_out = sem("u_out")
        y_ready = sem("y_ready")
        x2_done = sem("x2_done")
        x_centred = sem("x_centred")
        x2_centred = sem("x2_centred")
        xl_done = sem("xl_done")
        base_done = sem("base_done")
        xn_done = sem("xn_done")
        xnT_ready = sem("xnT_ready")
        xnT_out = sem("xnT_out")
        squared = sem("squared")
        dots_ready = sem("dots_ready")
        dots_taken = sem("dots_taken")
        onehot_done = sem("onehot_done")
        ranks_ready = sem("ranks_ready")
        ranks_taken = sem("ranks_taken")
        place_done = sem("place_done")
        scattered = sem("scattered")
        counts_ready = sem("counts_ready")
        pads_found = sem("pads_found")
        padded = sem("padded")
        tiles_found = sem("tiles_found")
        frow_in = [sem(f"frow{k}_in") for k in range(FB)]
        fxT_ready = sem("fxT_ready")
        fxT_hi_out = sem("fxT_hi_out")
        fxT_lo_out = sem("fxT_lo_out")
        up_split = sem("up_split")
        up_rest = sem("up_rest")
        up_ready = sem("up_ready")
        gated = sem("gated")
        act_done = sem("act_done")
        actT_ready = sem("actT_ready")
        actT_out = sem("actT_out")
        down_ready = sem("down_ready")
        fout_done = sem("fout_done")
        numbers_taken = sem("numbers_taken")
        settled = sem("settled")
        stored = [sem(f"out{k}_stored") for k in range(FB)]

        block = es.enter_context(nc.Block())

        def g_bank(h):
            return MISC if h % 2 else Y_BANK

        def y_bank(s):
            return MISC if isinstance(s, int) and s == TILES - 3 else Y_BANK

        def groups(eng, group):
            group(0, 0, False, True)
            with eng.Fori(0, LOOPS) as i:
                for k in range(2):
                    group(1 + k + 2 * i, (1 + k) % 2, True, True)
            group(GROUPS - 1, (GROUPS - 1) % 2, True, False)

        def ffn_pairs(eng, pair, drain=False):
            for k in range(0, FB, 2):
                pair(k, k, 0, k)
            with eng.Fori(1, FT // FB) as i:
                for k in range(0, FB, 2):
                    pair(FB * i + k, k, i, FB + k)
            if drain:
                for k in range(0, LAG, 2):
                    pair(FT + k, k, FT // FB, FT + k)

        def settle_v():
            return nc.vector.memset(spare_v[:], 0.0)

        def settle_p(column):
            return nc.gpsimd.tensor_tensor(spare_p[:, column:column + 1], part_f[:], part_f[:], ALU.add)

        class Chain:

            def __init__(self, eng, sem):
                self.eng, self.sem, self.base, self.n = eng, sem, 0, 0

            def mark(self, ins):
                ins.then_inc(self.sem, 1)
                self.n += 1

            def wait(self):
                self.eng.wait_ge(self.sem, self.base + self.n)

            def wait_for(self, n):
                self.eng.wait_ge(self.sem, self.base + n)

            def then(self, ins):
                self.mark(ins)
                self.wait()

            def loop(self, i, per_turn):
                self.start = self.n
                self.base, self.n = self.n + i * per_turn, 0
                self.per_turn = per_turn

            def end_loop(self, turns):
                assert self.n == self.per_turn, (self.n, self.per_turn)
                self.base, self.n = 0, self.start + turns * self.per_turn

        def pads(eng, experts):
            eng.wait_ge(pads_found, 1)
            for e in experts:
                row = eng.value_load(pad_i[0:1, e:e + 1], min_val=0, max_val=EXPERTS * REGION - P)
                eng.dma_start(table[bass.ds(row, P), :], pad_row[:]).then_inc(padded, 16)

        @block.sync
        def _(sp):
            sp.dma_start(xin[:], x_v[0]).then_inc(x_in, 16)
            sp.dma_start(wqT, wq_t.rearrange("(c p) d -> p c d", p=P)).then_inc(qk_weights_in, 16)
            sp.dma_start(wkT, wk_t.rearrange("(c p) d -> p c d", p=P)).then_inc(qk_weights_in, 16)
            sp.dma_start(xres[:, 1], x_v[1]).then_inc(x1_in, 16)
            sp.dma_start(ctxT[:, 0, :], ctxt_v[0]).then_inc(ctxT_in, 16)
            sp.dma_start(scale_b[:], scale.to_broadcast([P, D])).then_inc(small_in, 16)
            sp.dma_start(centT[:], cent_t).then_inc(small_in, 16)
            sp.dma_start(wvT, wv_t.rearrange("(c p) d -> p c d", p=P)).then_inc(vo_weights_in, 16)
            sp.dma_start(wo_sb, wo.rearrange("(c p) d -> p c d", p=P)).then_inc(vo_weights_in, 16)
            sp.dma_start(ctxN[:, 0], ctx_v[0]).then_inc(ctxN_in, 16)
            sp.dma_start(xres[:, 0], x_v[0]).then_inc(xres_in, 16)
            sp.dma_start(upw[:].rearrange("p (e h) -> p e h", e=EXPERTS),
                         up_w.rearrange("e d h -> d e h")).then_inc(ffn_in, 16)
            sp.dma_start(downw[:].rearrange("p (e c d) -> p e c d", e=EXPERTS, c=2),
                         down_w.rearrange("e (c p) d -> p e c d", p=P)).then_inc(ffn_in, 16)

            def group(g, par, has_prev, has_next):
                if not has_next:
                    return
                sp.wait_ge(ln1_done, g + 2)
                sp.dma_start(xin[:], x_v[(g + 2) % GROUPS]).then_inc(x_in, 16)
                if has_prev:
                    sp.wait_ge(x2_done, TPG * g)
                else:
                    sp.wait_ge(ctxT_in, 16)
                    sp.wait_ge(ctxN_in, 16)
                sp.dma_start(ctxT[:, 1 - par, :], ctxt_v[g + 1]).then_inc(ctxT_in, 16)
                sp.dma_start(ctxN[:, 1 - par], ctx_v[g + 1]).then_inc(ctxN_in, 16)
                if has_prev:
                    sp.wait_ge(x2_done, TPG * g + 1)
                    sp.dma_start(xres[:, 1 - par], x_v[g + 1]).then_inc(xres_in, 16)

            groups(sp, group)

            pads(sp, range(0, EXPERTS, 2))

            sp.wait_ge(tiles_found, 1)
            sp.wait_ge(padded, 16 * EXPERTS)
            sp.wait_ge(scattered, 16 * (TILES + 1))

            def pair(j, k, turn, static):
                for n in range(2):
                    if static >= FB:
                        sp.wait_ge(fout_done, j + n - FB + 1)
                        sp.wait_ge(numbers_taken, j + n - FB + 1)
                    row = sp.value_load(t_row[0:1, bass.ds(j + n, 1)], min_val=0,
                                        max_val=EXPERTS * REGION)
                    sp.dma_start(frow[:, k + n, :], table[bass.ds(row, P), :]).then_inc(frow_in[k + n], 16)

            ffn_pairs(sp, pair)

        @block.gpsimd
        def _(pool):
            seq = Chain(pool, pool_seq)
            nc.gpsimd.memset(ones_f[:], 1.0).then_inc(pool_seq, 1)
            nc.gpsimd.memset(ident[:], 0.0).then_inc(pool_seq, 1)
            nc.gpsimd.memset(id32f[:], 0.0).then_inc(pool_seq, 1)
            nc.gpsimd.memset(blk_f[:], 0.0).then_inc(pool_seq, 1)
            nc.gpsimd.memset(pad_row[:], 0.0).then_inc(pool_seq, 1)
            nc.gpsimd.memset(rows[:, :, :, ID_AT:], 0.0).then_inc(pool_seq, 1)
            seq.n = 6
            seq.wait()
            seq.mark(nc.gpsimd.affine_select(out=ident[:], in_=ident[:], compare_op=ALU.not_equal, fill=1.0,
                                             base=0, pattern=[[-1, P]], channel_multiplier=1))
            for q in range(P // BLK):
                seq.then(nc.gpsimd.affine_select(out=id32f[:], in_=id32f[:], compare_op=ALU.not_equal, fill=1.0,
                                                 base=-BLK * q, pattern=[[-1, BLK]], channel_multiplier=1))
            for q in range(P // SEQ):
                seq.then(nc.gpsimd.memset(blk_f[q * SEQ:(q + 1) * SEQ, q * SEQ:(q + 1) * SEQ], 1.0))
            nc.gpsimd.memset(power[:], -0.5).then_inc(consts_made, 1)
            pool.wait_ge(consts_made, 1)

            def root_x(g):
                pool.wait_ge(var1_done, g + 1)
                nc.gpsimd.tensor_tensor(rstd1[:], var1[:], power[:, 0:TPG], ALU.pow).then_inc(rstd1_done, 1)

            def per_row(ap):
                return ap.unsqueeze(2).to_broadcast([P, TPG, D])

            def norm_x(g, src):
                if not (isinstance(g, int) and g == 0):
                    pool.wait_ge(xT_ready, g)
                nc.gpsimd.tensor_tensor(xln[:], src, per_row(mv1[:, :, 0]), ALU.subtract).then_inc(x_centred, 1)
                pool.wait_ge(rstd1_done, g + 1)
                pool.wait_ge(x_centred, g + 1)
                nc.gpsimd.tensor_tensor(xln[:], xln[:], per_row(rstd1[:]), ALU.mult).then_inc(ln1_done, 1)

            def root_x2(g):
                pool.wait_ge(spread2_done, g + 1)
                nc.gpsimd.tensor_tensor(root2[:].rearrange("p a t -> p (a t)"),
                                        spread2[:].rearrange("p a t -> p (a t)"), power[:],
                                        ALU.pow).then_inc(root2_done, 1)

            def norm_x2(g):
                nc.gpsimd.tensor_tensor(xl[:], x2[:], per_row(mv2[:, :, 0]), ALU.subtract).then_inc(x2_centred, 1)
                pool.wait_ge(root2_done, g + 1)
                pool.wait_ge(x2_centred, g + 1)
                nc.gpsimd.tensor_tensor(xl[:], xl[:], per_row(root2[:, 0, :]), ALU.mult).then_inc(xl_done, 1)

            root_x(0)
            norm_x(0, xin[:])

            seq.mark(nc.gpsimd.iota(expert_m8[:], pattern=[[1, EXPERTS]], base=-EXPERTS, channel_multiplier=0,
                                    allow_small_or_imprecise_dtypes=True))
            seq.mark(nc.gpsimd.iota(region_of[:], pattern=[[REGION, EXPERTS]], base=0, channel_multiplier=0,
                                    allow_small_or_imprecise_dtypes=True))
            seq.mark(nc.gpsimd.iota(token_f[:], pattern=[[P, TPG]], base=0, channel_multiplier=1,
                                    allow_small_or_imprecise_dtypes=True))
            seq.mark(nc.gpsimd.iota(part_f[:], pattern=[[0, 1]], base=0, channel_multiplier=1,
                                    allow_small_or_imprecise_dtypes=True))
            seq.mark(nc.gpsimd.iota(tile_no[:], pattern=[[1, FT]], base=0, channel_multiplier=0,
                                    allow_small_or_imprecise_dtypes=True))
            seq.mark(nc.gpsimd.memset(pad_row[:, ID_AT:ID_AT + 1], float(NO_TOKEN)))
            seq.mark(nc.gpsimd.memset(upto[:], 1.0))
            seq.mark(nc.gpsimd.memset(before_b[:], 1.0))
            seq.wait()
            seq.mark(nc.gpsimd.affine_select(out=upto[:], in_=upto[:], compare_op=ALU.is_ge, fill=0.0, base=0,
                                             pattern=[[1, EXPERTS], [-1, EXPERTS]], channel_multiplier=0))
            seq.mark(nc.gpsimd.affine_select(out=before_b[:], in_=before_b[:], compare_op=ALU.is_gt, fill=0.0,
                                             base=0, pattern=[[1, P]], channel_multiplier=-1))
            seq.wait()
            nc.gpsimd.memset(seen[:], 0.0).then_inc(consts_made, 1)
            pool.dma_start(table[EXPERTS * REGION:, :], pad_row[:]).then_inc(scattered, 16)
            def spread_max(s, par):
                pool.wait_ge(max_found, 3 * (s + 1))
                if not (isinstance(s, int) and s < 2):
                    pool.wait_ge(shifted, s - 1)
                nc.gpsimd.tensor_tensor(
                    max_rows[:, par].rearrange("p (b j) -> p b j", j=BLK),
                    neg_max[:, par].unsqueeze(2).to_broadcast([P, NBLK, BLK]),
                    id32b[:].unsqueeze(1).to_broadcast([P, NBLK, BLK]), ALU.mult).then_inc(max_spread, 1)

            def spread_inv(s, par):
                pool.wait_ge(inv_found, 2 * (s + 1))
                if not (isinstance(s, int) and s < 2):
                    pool.wait_ge(inv_ready, 2 * (s - 1))
                nc.gpsimd.tensor_tensor(
                    inv_rows[:, par].rearrange("p (b j) -> p b j", j=BLK),
                    inv[:, par].unsqueeze(2).to_broadcast([P, NBLK, BLK]),
                    id32f[:].unsqueeze(1).to_broadcast([P, NBLK, BLK]), ALU.mult).then_inc(inv_spread, 1)

            def residual(g, par):
                pool.wait_ge(xl_done, g + 1)
                nc.gpsimd.tensor_tensor(rows[:, par, :, D:2 * D], x2[:], xl[:], ALU.add).then_inc(base_done, 1)
                nc.gpsimd.tensor_copy(rows[:, par, :, ID_AT:ID_AT + 1],
                                      token_f[:].unsqueeze(2)).then_inc(base_done, 1)
                pool.wait_ge(base_done, 3 * g + 2)
                settle_p(0)
                nc.gpsimd.tensor_scalar(token_f[:], token_f[:], float(GT), None, ALU.add).then_inc(base_done, 1)

            def scatter(g, par):
                pool.wait_ge(place_done, g + 1)
                pool.wait_ge(xn_done, TPG * (g + 1))
                pool.wait_ge(base_done, 3 * (g + 1))
                settle_p(1)
                for t in range(TPG):
                    pool.indirect_dma_start(
                        out=table[:, :], out_offset=bass.IndirectOffsetOnAxis(ap=place_u[:, par, t:t + 1], axis=0),
                        in_=rows[:, par, t, :], in_offset=None).then_inc(scattered, 16)

            def group(g, par, has_prev, has_next):
                for t in range(TPG):
                    s = TPG * g + t
                    if t == 1 and has_next:
                        root_x(g + 2)
                        norm_x(g + 2, xin[:])
                    if has_prev and t == (2 if has_next else 3):
                        root_x2(g - 1)
                        norm_x2(g - 1)
                        residual(g - 1, 1 - par)
                    max_first = t == 1 and not has_prev
                    if (t >= 2 or has_prev) and not max_first:
                        spread_inv(s - 1, (t + 1) % 2)
                    spread_max(s, t % 2)
                    if max_first:
                        spread_inv(s - 1, 0)
                    if t == 3 and has_prev and has_next:
                        scatter(g - 1, 1 - par)

            pool.wait_ge(consts_cast, 1)
            root_x(1)
            norm_x(1, xres[:, 1])
            groups(pool, group)
            spread_inv(TILES - 1, 1)
            last = GROUPS - 1
            scatter(last - 1, 1 - last % 2)
            root_x2(last)
            residual(last, last % 2)
            scatter(last, last % 2)

            def pair(j, k, turn, static):
                for n in range(2):
                    pool.wait_ge(fout_done, j + n + 1)
                    pool.wait_ge(numbers_taken, j + n + 1)
                    if static or n:
                        pool.wait_ge(settled, j + n)
                    settle_p(2).then_inc(settled, 1)
                    pool.indirect_dma_start(
                        out=out, out_offset=bass.IndirectOffsetOnAxis(ap=numbers[:, k + n:k + n + 1], axis=0),
                        in_=fout[:, k + n, :], in_offset=None, bounds_check=TOKENS - 1,
                        oob_is_err=False).then_inc(stored[k + n], 16)

            ffn_pairs(pool, pair)
            for k in range(FB):
                pool.wait_ge(stored[k], 16 * (FT // FB))

        @block.tensor
        def _(pe):
            mm = nc.tensor.matmul

            def fold(left, right, q, pair):
                for h in (4 * q, 4 * q + 2, 4 * q + 1, 4 * q + 3):
                    r = HD * (h % 2)
                    at = ((h // 2) % 2) * D
                    last = mm(pair[h % 2][:, at:at + D], left[r:r + HD, h // 2, :], right[r:r + HD, h // 2, :],
                              start=True, stop=True, skip_group_check=True)
                last.then_inc(fold_ready, 1)

            def fold_m(q):
                if q == 0:
                    pe.wait_ge(vo_weights_in, 32)
                    pe.wait_ge(a_rest, 8)
                else:
                    pe.wait_ge(m_copied, 2 * q)
                fold(wvT, wo_sb, q, FOLD_BANKS[2])

            def stay_awake(n):
                for _ in range(n):
                    mm(S_BANK[0][0][:, :], ones_b[:], max_rows[:, 0, 0:HALF], start=True, stop=True)

            def turn_x(g, bank=MISC):
                pe.wait_ge(ln1_done, g + 1)
                for t in range(TPG):
                    last = nc.tensor.transpose(bank[:, t * P:(t + 1) * P], xln[:, t, :], ident[:])
                last.then_inc(xT_ready, 1)

            def queries(h, par):
                for n, (a, b) in enumerate(((a_hi, xT_hi), (a_lo, xT_hi), (a_hi, xT_lo))):
                    last = mm(g_bank(h)[:, :], a[:, h, :], b[:, par], start=(n == 0), stop=(n == 2))
                last.then_inc(g_ready, 1)

            def scores(s, t, par):
                for half in range(2):
                    if half and isinstance(s, int) and s == 0:
                        pe.wait_ge(g_out, HEADS)
                    for b in range(2):
                        last = mm(S_BANK[t % 2][half][b * SEQ:(b + 1) * SEQ, :],
                                  ctxT[:, par, t * P + b * SEQ:t * P + (b + 1) * SEQ],
                                  gq[:, par, 8 * half:8 * half + 8, t * P + b * SEQ:t * P + (b + 1) * SEQ],
                                  start=True, stop=True, skip_group_check=True)
                last.then_inc(scores_ready, 1)

            def shift(s, b):
                pe.wait_ge(max_spread, s + 1)
                for half in range(2):
                    last = mm(S_BANK[b][half][:, :], blk_b[:], max_rows[:, b, half * HALF:(half + 1) * HALF],
                              start=False, stop=True, skip_group_check=True)
                last.then_inc(shifted, 1)

            def spread(s, b, half):
                if half == 0:
                    pe.wait_ge(inv_spread, s + 1)
                else:
                    pe.wait_ge(probs_ready, 2 * s + 1)
                mm(R_BANK[:, :], blk_r[:], inv_rows[:, b, half * HALF:(half + 1) * HALF],
                   start=True, stop=True).then_inc(inv_ready, 1)

            def values(s, t, par, b2, n):
                half, b = n // 2, n % 2
                if n == 0:
                    pe.wait_ge(probs_ready, 2 * s + 1)
                if n == 1:
                    pe.wait_ge(probs_ready, 2 * (s + 1))
                if n >= 2:
                    pe.wait_ge(u_out, 4 * s + n - 1)
                mm(VALUES_BANK[b][:, :], ctxN[b * SEQ:(b + 1) * SEQ, par, t, :],
                   probs[b * SEQ:(b + 1) * SEQ, b2, half * HALF:(half + 1) * HALF],
                   start=True, stop=True).then_inc(u_ready, 1)

            def project(s, b2, half):
                pe.wait_ge(u_out, 4 * s + 2 * (half + 1))
                for h in range(HEADS // 2 * half, HEADS // 2 * (half + 1)):
                    last = mm(y_bank(s)[:, 0:D], ut[:, b2, h, :], m_sb[:, h, :], start=(h == 0), stop=(h == HEADS - 1))
                if half:
                    last.then_inc(y_ready, 1)

            def turn_normed(g, par):
                pe.wait_ge(xn_done, TPG * (g + 1))
                for t in range(TPG):
                    last = nc.tensor.transpose(MISC[:, t * P:(t + 1) * P], rows[:, par, t, 0:D], ident[:])
                last.then_inc(xnT_ready, 1)

            def dots(g):
                pe.wait_ge(xnT_out, g + 1)
                for t in range(TPG):
                    last = mm(MISC[:, t * EXPERTS:(t + 1) * EXPERTS], xnT[:, t * P:(t + 1) * P], centT[:],
                              start=True, stop=True)
                last.then_inc(dots_ready, 1)

            def ranks(g):
                pe.wait_ge(onehot_done, g + 1)
                n = TPG * EXPERTS
                mm(MISC[:, 0:n], before_b[:], onehot[:].rearrange("p t e -> p (t e)"), start=True, stop=False)
                for t in range(TPG - 1):
                    mm(MISC[:, (t + 1) * EXPERTS:n].rearrange("p (t e) -> p t e", e=EXPERTS), ones_b[:],
                       onehot[:, t:t + 1, :].to_broadcast([P, TPG - 1 - t, EXPERTS]), start=False, stop=False,
                       skip_group_check=True)
                mm(MISC[:, 0:n].rearrange("p (t e) -> p t e", e=EXPERTS), ones_b[:],
                   seen[:].unsqueeze(1).to_broadcast([P, TPG, EXPERTS]),
                   start=False, stop=True).then_inc(ranks_ready, 1)

            pe.wait_ge(qk_weights_in, 32)
            for q in range(HEADS // 4):
                if q == 2:
                    turn_x(0)
                if q == 3:
                    pe.wait_ge(a_rest, 2)
                fold(wqT, wkT, q, FOLD_BANKS[q % 3])
            pe.wait_ge(xT_hi_out, 1)
            pe.wait_ge(xT_lo_out, 1)
            for h in range(HEADS):
                if h % 4 == 0:
                    pe.wait_ge(a_rest, h // 2 + 2)
                if h >= 2:
                    pe.wait_ge(g_out, h - 1)
                queries(h, 0)
                if h == HEADS // 2:
                    turn_x(1, U_BANK)
                    pe.wait_ge(norm_squares, 1)
                    mm(R_BANK[:, 0:EXPERTS], ones_f[:], cent_sq[:], start=True, stop=True).then_inc(norm_ready, 1)
            pe.wait_ge(xT_hi_out, 2)
            pe.wait_ge(xT_lo_out, 2)
            pe.wait_ge(norm_taken, 1)
            pe.wait_ge(ctxT_in, 16)
            pe.wait_ge(ctxN_in, 16)

            def next_head(g, par, has_prev, t, place):
                h = HEADS_PER_STEP * t + place
                if place == 0 and (t == 3 or has_prev):
                    pe.wait_ge(x2_done, TPG * g + t - 2)
                elif place == 1 and t == 2:
                    pe.wait_ge(xT_hi_out, g + 3)
                    pe.wait_ge(xT_lo_out, g + 3)
                elif place == 1 and t == 3 and has_prev:
                    pe.wait_ge(dots_taken, g)
                elif place == 3 and t == 3 and has_prev:
                    pe.wait_ge(ranks_taken, g)
                elif h >= 2:
                    pe.wait_ge(g_out, HEADS * (g + 1) + h - 1)
                queries(h, 1 - par)

            def group(g, par, has_prev, has_next):
                for t in range(TPG):
                    s = TPG * g + t
                    if t == 0:
                        if has_prev:
                            pe.wait_ge(g_out, HEADS * (g + 1))
                        pe.wait_ge(ctxT_in, 16 * (g + 1))
                        pe.wait_ge(ctxN_in, 16 * (g + 1))
                    if t >= 2 or has_prev:
                        pe.wait_ge(exp_done, 2 * (s - 1))
                    if t == 1 and not has_prev:
                        shift(s - 1, 0)
                    else:
                        scores(s, t, par)
                    if t == 3 and has_prev and has_next:
                        pe.wait_ge(g_out, HEADS * (g + 1) + HEADS_PER_STEP * t)
                        turn_normed(g - 1, 1 - par)
                    tv, pv = (t - 2, par) if t >= 2 else (t + 2, 1 - par)
                    if t == 2 and not has_prev:
                        pe.wait_ge(m_copied, HEADS // 2)
                    if t >= 2 or has_prev:
                        spread(s - 2, t % 2, 0)
                    if has_next:
                        next_head(g, par, has_prev, t, 0)
                    if t == 3 and has_prev and has_next:
                        dots(g - 1)
                    if t == 3 or has_prev:
                        shift(s - 1, (t + 1) % 2)
                    if t >= 2 or has_prev:
                        spread(s - 2, t % 2, 1)
                    if t == 1 and not has_prev:
                        fold_m(2)
                    if has_next:
                        next_head(g, par, has_prev, t, 1)
                    if t >= 2 or has_prev:
                        values(s - 2, tv, pv, t % 2, 0)
                        values(s - 2, tv, pv, t % 2, 1)
                    if has_next:
                        next_head(g, par, has_prev, t, 2)
                    if t >= 2 or has_prev:
                        values(s - 2, tv, pv, t % 2, 2)
                        values(s - 2, tv, pv, t % 2, 3)
                    if t == 3 and has_prev and has_next:
                        pe.wait_ge(g_out, HEADS * (g + 1) + HEADS_PER_STEP * t + 2)
                        ranks(g - 1)
                    if t >= 2 or has_prev:
                        if has_next:
                            pe.wait_ge(g_out, HEADS * (g + 1) + HEADS_PER_STEP * t + 3)
                        elif s < TILES - 1:
                            pe.wait_ge(x2_done, s - 2)
                        project(s - 2, t % 2, 0)
                    if has_next:
                        next_head(g, par, has_prev, t, 3)
                    if t == 0 and not has_prev:
                        scores(s + 1, 1, par)
                        fold_m(0)
                        fold_m(1)
                    if t == 1 and not has_prev:
                        fold_m(3)
                    if t >= 2 or has_prev:
                        project(s - 2, t % 2, 1)
                    if t == 1 and has_next:
                        pe.wait_ge(g_out, HEADS * (g + 1) + HEADS_PER_STEP * (t + 1))
                        turn_x(g + 2)
                    if t == 1 and not has_prev:
                        shift(s, 1)

            groups(pe, group)
            last = GROUPS - 1
            spread(TILES - 2, 0, 0)
            spread(TILES - 2, 0, 1)
            for n in range(4):
                if n == 2:
                    shift(TILES - 1, 1)
                values(TILES - 2, TPG - 2, last % 2, 0, n)
            pe.wait_ge(x2_done, TILES - 3)
            project(TILES - 2, 0, 0)
            pe.wait_ge(x2_done, TILES - 2)
            turn_normed(last - 1, 1 - last % 2)
            project(TILES - 2, 0, 1)
            dots(last - 1)
            stay_awake(4)
            pe.wait_ge(u_out, 4 * (TILES - 1))
            spread(TILES - 1, 1, 0)
            stay_awake(6)
            spread(TILES - 1, 1, 1)
            pe.wait_ge(dots_taken, last)
            ranks(last - 1)
            for n in range(4):
                values(TILES - 1, TPG - 1, last % 2, 1, n)
            pe.wait_ge(x2_done, TILES - 1)
            project(TILES - 1, 1, 0)
            project(TILES - 1, 1, 1)
            stay_awake(24)
            pe.wait_ge(ranks_taken, last)
            turn_normed(last, last % 2)
            dots(last)
            pe.wait_ge(dots_taken, last + 1)
            ranks(last)
            pe.wait_ge(place_done, last + 1)
            mm(MISC[:, 0:EXPERTS], ones_b[:], seen[:], start=True, stop=True).then_inc(counts_ready, 1)

            pe.wait_ge(tiles_found, 1)
            pe.wait_ge(up_rest, UP_PIECES)
            stay_awake(20)

            def pair(j, k, turn, static):
                if static < FT:
                    for n in range(2):
                        pe.wait_ge(frow_in[k + n], 16 * (turn + 1))
                        last = nc.tensor.transpose(TURN_BANK[:, n * P:(n + 1) * P], frow[:, k + n, 0:D], ident[:])
                    last.then_inc(fxT_ready, 1)
                four = pe.value_load(t_experts[0:1, bass.ds(FB // 2 * turn + k // 2, 1)], min_val=0,
                                     max_val=EXPERTS ** 4 - 1)
                e = [(four // EXPERTS ** n) % EXPERTS for n in range(4)]
                if static >= LAG:
                    for n in range(2):
                        pe.wait_ge(actT_out, j + n - LAG + 1)
                        if static >= LAG + 2:
                            pe.wait_ge(fout_done, j + n - LAG - 1)
                        for c in range(2):
                            last = mm(DOWN_BANK[n][:, 0:D], actT[:, n, c * P:(c + 1) * P],
                                      downw[:, bass.ds(e[n] * (2 * D) + c * D, D)], start=(c == 0), stop=(c == 1))
                        last.then_inc(down_ready, 1)
                if 2 <= static < FT + 2:
                    for n in range(2):
                        pe.wait_ge(act_done, j + n - 1)
                        for c in range(2):
                            last = nc.tensor.transpose(ACT_BANK[n][:, c * P:(c + 1) * P],
                                                       act[:, n, c * P:(c + 1) * P], ident[:])
                        last.then_inc(actT_ready, 1)
                if static < FT:
                    pe.wait_ge(fxT_hi_out, FB // 2 * turn + k // 2 + 1)
                    pe.wait_ge(fxT_lo_out, FB // 2 * turn + k // 2 + 1)
                    for n in range(2):
                        for m, (a, b) in enumerate(((fxT_hi, up_hi), (fxT_hi, up_lo), (fxT_lo, up_hi))):
                            last = mm(UP_BANK[n][:, :], a[:, n * P:(n + 1) * P],
                                      b[:, bass.ds(e[2 + n] * (2 * HID), 2 * HID)], start=(m == 0), stop=(m == 2))
                        last.then_inc(up_ready, 1)

            ffn_pairs(pe, pair, drain=True)

        @block.scalar
        def _(sc):
            copy = nc.scalar.copy

            def fold_out(n, q, pair, dst, sem):
                sc.wait_ge(fold_ready, n)
                for r in range(2):
                    copy(dst[:, 4 * q + r:4 * q + r + 3:2, :],
                         pair[r][:, 0:2 * D].rearrange("p (k d) -> p k d", k=2)).then_inc(sem, 1)

            def m_out(q):
                fold_out(HEADS // 4 + q + 1, q, FOLD_BANKS[2], m_sb, m_copied)

            def turned_x(g, par, bank=MISC):
                sc.wait_ge(xT_ready, g + 1)
                copy(xT_hi[:, par], bank[:]).then_inc(xT_hi_out, 1)

            def queries_out(g, h, par):
                sc.wait_ge(g_ready, HEADS * g + h + 1)
                copy(gq[:, par, h, :], g_bank(h)[:]).then_inc(g_out, 1)

            def take_dots(g):
                sc.wait_ge(dots_ready, g + 1)
                copy(dot[:], MISC[:, 0:TPG * EXPERTS]).then_inc(dots_taken, 1)

            def square_rows(g, par):
                sc.wait_ge(xn_done, TPG * (g + 1))
                for t in range(TPG):
                    nc.scalar.activation(square[:, t, :], rows[:, par, t, 0:D], ACT.Square,
                                         accum_out=norm2[:, t:t + 1]).then_inc(squared, 1)

            def take_ranks(g):
                sc.wait_ge(ranks_ready, g + 1)
                copy(rank[:], MISC[:, 0:TPG * EXPERTS]).then_inc(ranks_taken, 1)

            def exps(s, b):
                sc.wait_ge(shifted, s + 1)
                for half in range(2):
                    nc.scalar.activation(probs[:, b, half * HALF:(half + 1) * HALF], S_BANK[b][half][:],
                                         ACT.Exp, scale=SCORE_SCALE).then_inc(exp_done, 1)

            def values_out(s, b2, n):
                half, b = n // 2, n % 2
                if n == 0 and not (isinstance(s, int) and s < 2):
                    sc.wait_ge(y_ready, s - 1)
                sc.wait_ge(u_ready, 4 * s + n + 1)
                copy(ut[:, b2, 8 * half:8 * half + 8, b * SEQ:(b + 1) * SEQ],
                     VALUES_BANK[b][:].rearrange("p (h q) -> p h q", q=SEQ)).then_inc(u_out, 1)

            def normed_out(g):
                sc.wait_ge(xnT_ready, g + 1)
                copy(xnT[:], MISC[:]).then_inc(xnT_out, 1)

            for q in range(HEADS // 4):
                if q == 2:
                    turned_x(0, 0)
                fold_out(q + 1, q, FOLD_BANKS[q % 3], a_hi, a_split)
            for h in range(HEADS):
                queries_out(0, h, 0)
                if h == HEADS // 2:
                    turned_x(1, 1, U_BANK)

            def group(g, par, has_prev, has_next):
                for t in range(TPG):
                    s = TPG * g + t
                    valued = t >= 2 or has_prev

                    def head(place):
                        if has_next:
                            queries_out(g + 1, HEADS_PER_STEP * t + place, 1 - par)

                    if t == 3 and has_prev and has_next:
                        square_rows(g - 1, 1 - par)
                        normed_out(g - 1)
                    if t == 1 and not has_prev:
                        exps(s - 1, 0)
                    head(0)
                    if t == 3 and has_prev and has_next:
                        take_dots(g - 1)
                    if t == 3 or has_prev:
                        exps(s - 1, (t + 1) % 2)
                    if t == 1 and not has_prev:
                        m_out(2)
                    head(1)
                    if valued:
                        values_out(s - 2, t % 2, 0)
                        values_out(s - 2, t % 2, 1)
                    head(2)
                    if valued:
                        values_out(s - 2, t % 2, 2)
                        values_out(s - 2, t % 2, 3)
                    if t == 3 and has_prev and has_next:
                        take_ranks(g - 1)
                    head(3)
                    if t == 0 and not has_prev:
                        m_out(0)
                        m_out(1)
                    if t == 1 and not has_prev:
                        m_out(3)
                    if t == 1 and has_next:
                        turned_x(g + 2, par)
                    if t == 1 and not has_prev:
                        exps(s, 1)
                    if t == 0 and not has_next:
                        sc.wait_ge(ffn_in, 32)
                        for n in range(UP_PIECES):
                            r = slice(n * UP_PIECE, (n + 1) * UP_PIECE)
                            copy(up_hi[:, r], upw[:, r]).then_inc(up_split, 1)

            groups(sc, group)
            for n in range(4):
                if n == 2:
                    exps(TILES - 1, 1)
                values_out(TILES - 2, 0, n)
            normed_out(GROUPS - 2)
            square_rows(GROUPS - 2, GROUPS % 2)
            take_dots(GROUPS - 2)
            take_ranks(GROUPS - 2)
            for n in range(4):
                values_out(TILES - 1, 1, n)
            normed_out(GROUPS - 1)
            square_rows(GROUPS - 1, (GROUPS - 1) % 2)
            take_dots(GROUPS - 1)
            take_ranks(GROUPS - 1)
            pads(sc, range(1, EXPERTS, 2))
            nc.scalar.activation(spare_s[:], part_f[:], ACT.Silu)

            def pair(j, k, turn, static):
                if static < FT:
                    sc.wait_ge(fxT_ready, FB // 2 * turn + k // 2 + 1)
                    copy(fxT_hi[:], TURN_BANK[:, 0:2 * P]).then_inc(fxT_hi_out, 1)
                if 2 <= static < FT + 2:
                    for n in range(2):
                        sc.wait_ge(actT_ready, j + n - 1)
                        copy(actT[:, n, :], ACT_BANK[n][:, 0:HID]).then_inc(actT_out, 1)
                if static < FT:
                    for n in range(2):
                        sc.wait_ge(up_ready, j + n + 1)
                        nc.scalar.activation(gate[:, n, :], UP_BANK[n][:, HID:2 * HID], ACT.Silu).then_inc(gated, 1)

            ffn_pairs(sc, pair, drain=True)

        @block.vector
        def _(dve):
            v = nc.vector
            seq = Chain(dve, dve_seq)

            def gather(src, stats, tiles):
                for t in tiles:
                    seq.mark(v.bn_stats(stats[:, t, :], src[:, t, :]))

            def statistics(src, stats, mv, gathered=0):
                gather(src, stats, range(gathered, TPG))
                seq.wait()
                settle_v()
                for t in range(TPG):
                    seq.mark(v.bn_aggr(mv[:, t, :], stats[:, t, :]))
                seq.wait()

            def measure_x(src, g):
                if not (isinstance(g, int) and g == 0):
                    dve.wait_ge(ln1_done, g)
                statistics(src, stats1, mv1)
                v.tensor_scalar(var1[:], mv1[:, :, 1], LN_EPS, None, ALU.add).then_inc(var1_done, 1)

            def split_x(g, par, bank=MISC):
                dve.wait_ge(xT_hi_out, g + 1)
                v.tensor_tensor(xT_lo[:, par], bank[:], xT_hi[:, par].bitcast(F32), ALU.subtract).then_inc(xT_lo_out, 1)

            def over_keys(dst, src, op):
                seq.mark(v.tensor_reduce(dst, src[:].rearrange("p (b k) -> p b k", k=BLK), AX_X, op))

            def other_half(n):
                for q in range(P // BLK):
                    seq.mark(v.tensor_copy(others[q * BLK:(q + 1) * BLK, n],
                                           keys[(q ^ 1) * BLK:((q ^ 1) + 1) * BLK, n]))

            def turn_scores(b, piece):
                half, at = piece // 2, piece % 2 * (HALF // 2)
                seq.mark(v.transpose(turned[:, piece * (HALF // 2):(piece + 1) * (HALF // 2)],
                                     S_BANK[b][half][:, at:at + HALF // 2]))

            def reduce_keys(s_sum, s_max, b, between=None):
                pieces = iter(range(4) if s_max is not None else ())

                def fill():
                    piece = next(pieces, None)
                    if piece is not None:
                        if piece == 0:
                            dve.wait_ge(scores_ready, s_max + 1)
                        turn_scores(b, piece)

                if s_sum is not None:
                    for half in range(2):
                        dve.wait_ge(exp_done, 2 * s_sum + half + 1)
                        r = slice(half * HALF, (half + 1) * HALF)
                        seq.mark(v.transpose(turned_p[:, r], probs[:, 1 - b, r]))
                    seq.wait()
                    over_keys(keys[:, 0], turned_p, ALU.add)
                    step = seq.n
                    fill()
                    seq.wait_for(step)
                    other_half(0)
                    step = seq.n
                    fill()
                    seq.wait_for(step)
                    seq.mark(v.tensor_tensor(total[:], keys[:, 0], others[:, 0], ALU.add))
                    step = seq.n
                    fill()
                    seq.wait_for(step)
                    if not (isinstance(s_sum, int) and s_sum < 2):
                        dve.wait_ge(inv_spread, s_sum - 1)
                    seq.mark(v.reciprocal(inv[:, 1 - b], total[:]))
                    step = seq.n
                    fill()
                    seq.wait_for(step)
                    seq.then(v.tensor_copy(inv_hi[:], inv[:, 1 - b]))
                    for q in (1, 3):
                        r = slice(q * BLK, (q + 1) * BLK)
                        v.tensor_tensor(inv[r, 1 - b], inv[r, 1 - b], inv_hi[r, :].bitcast(F32),
                                        ALU.subtract).then_inc(inv_found, 1)
                else:
                    for _ in range(4):
                        fill()
                if between is not None:
                    between()
                if s_max is not None:
                    seq.wait()
                    over_keys(keys[:, 1], turned, ALU.max)
                    seq.wait()
                    other_half(1)
                    seq.wait()
                    seq.then(v.tensor_tensor(top[:], keys[:, 1], others[:, 1], ALU.max))
                    if not (isinstance(s_max, int) and s_max < 2):
                        dve.wait_ge(max_spread, s_max - 1)
                    v.tensor_scalar(neg_max[:, b], top[:], -1.0, None, ALU.mult).then_inc(max_found, 1)
                    dve.wait_ge(max_found, 3 * s_max + 1)
                    for q in (1, 3):
                        r = slice(q * BLK, (q + 1) * BLK)
                        v.scalar_tensor_tensor(out=neg_max[r, b], in0=top[r, :], scalar=-1.0, in1=neg_max[r, b],
                                               op0=ALU.mult, op1=ALU.subtract).then_inc(max_found, 1)

            def normalise(s, b):
                for half in range(2):
                    dve.wait_ge(inv_ready, 2 * s + half + 1)
                    r = slice(half * HALF, (half + 1) * HALF)
                    v.tensor_tensor(probs[:, b, r], probs[:, b, r], R_BANK[:],
                                    ALU.mult).then_inc(probs_ready, 1)

            def add_residual(s, g, t, par):
                dve.wait_ge(y_ready, s + 1)
                if t == 0:
                    if not (isinstance(s, int) and s == 0):
                        dve.wait_ge(base_done, 3 * g)
                        dve.wait_ge(xres_in, 16 * g)
                    else:
                        dve.wait_ge(xres_in, 16)
                v.tensor_tensor(x2[:, t, :], y_bank(s)[:, 0:D], xres[:, par, t, :], ALU.add).then_inc(x2_done, 1)

            def measure_x2(g, gathered=0):
                dve.wait_ge(x2_done, TPG * (g + 1))
                statistics(x2, stats2, mv2, gathered)
                var = mv2[:, :, 1]
                seq.then(v.tensor_scalar(spread2[:, 0, :], var, LN_EPS, None, ALU.add))
                seq.then(v.reciprocal(var_inv[:], spread2[:, 0, :]))
                seq.then(v.tensor_tensor(var_inv[:], var, var_inv[:], ALU.mult))
                v.tensor_scalar(spread2[:, 1, :], var_inv[:], RMS_EPS, None, ALU.add).then_inc(spread2_done, 1)

            def scaled(g, par):
                dve.wait_ge(xl_done, g + 1)
                dve.wait_ge(scattered, 16 * (TPG * g + 1))
                for t in range(TPG):
                    v.scalar_tensor_tensor(out=rows[:, par, t, 0:D], in0=xl[:, t, :], scalar=root2[:, 1, t:t + 1],
                                           in1=scale_b[:], op0=ALU.mult, op1=ALU.mult).then_inc(xn_done, 1)

            def add_norms(g):
                dve.wait_ge(squared, TPG * (g + 1))
                seq.then(v.tensor_tensor(norms[:], norm2[:].unsqueeze(2).to_broadcast([P, TPG, EXPERTS]),
                                         cent_norm[:].unsqueeze(1).to_broadcast([P, TPG, EXPERTS]), ALU.add))

            def choose(g):
                def experts(ap):
                    return ap.unsqueeze(1).to_broadcast([P, TPG, EXPERTS])

                dve.wait_ge(dots_taken, g + 1)
                seq.then(v.scalar_tensor_tensor(out=dist[:].rearrange("p t e -> p (t e)"), in0=dot[:],
                                                scalar=-2.0, in1=norms[:].rearrange("p t e -> p (t e)"),
                                                op0=ALU.mult, op1=ALU.add))
                seq.then(v.tensor_reduce(least[:], dist[:], AX_X, ALU.min))
                seq.then(v.tensor_tensor(cand[:], dist[:], least[:].unsqueeze(2).to_broadcast([P, TPG, EXPERTS]),
                                         ALU.is_le))
                seq.then(v.tensor_tensor(cand[:], cand[:], experts(expert_m8[:]), ALU.mult))
                seq.then(v.tensor_reduce(chosen[:], cand[:], AX_X, ALU.min))
                v.tensor_tensor(onehot[:], experts(expert_m8[:]),
                                chosen[:].unsqueeze(2).to_broadcast([P, TPG, EXPERTS]),
                                ALU.is_equal).then_inc(onehot_done, 1)

            def places(g, par):
                dve.wait_ge(ranks_taken, g + 1)
                seq.then(v.tensor_tensor(place[:], rank[:].rearrange("p (t e) -> p t e", e=EXPERTS),
                                         region_of[:].unsqueeze(1).to_broadcast([P, TPG, EXPERTS]), ALU.add))
                seq.mark(v.tensor_tensor(place[:], place[:], onehot[:], ALU.mult))
                seq.then(v.tensor_reduce(chose[:], onehot[:].rearrange("p t e -> p e t"), AX_X, ALU.add))
                seq.mark(v.tensor_tensor(seen[:], seen[:], chose[:], ALU.add))
                seq.then(v.tensor_reduce(place_f[:], place[:], AX_X, ALU.add))
                v.tensor_copy(place_u[:, par, :], place_f[:]).then_inc(place_done, 1)

            def split_up(pieces):
                for n in pieces:
                    dve.wait_ge(up_split, n + 1)
                    r = slice(n * UP_PIECE, (n + 1) * UP_PIECE)
                    v.tensor_tensor(up_lo[:, r], upw[:, r], up_hi[:, r].bitcast(F32),
                                    ALU.subtract).then_inc(up_rest, 1)

            dve.wait_ge(x_in, 16)
            measure_x(xin, 0)
            dve.wait_ge(consts_made, 1)
            v.tensor_copy(id32b[:], id32f[:])
            v.tensor_copy(blk_b[:], blk_f[:])
            v.tensor_copy(blk_r[:], blk_f[:])
            v.tensor_copy(ones_b[:], ones_f[:]).then_inc(consts_cast, 1)
            for q in range(HEADS // 4):
                if q == 2:
                    split_x(0, 0)
                dve.wait_ge(a_split, 2 * q + 2)
                for r in range(2):
                    v.tensor_tensor(a_lo[:, 4 * q + r:4 * q + r + 3:2, :],
                                    FOLD_BANKS[q % 3][r][:, 0:2 * D].rearrange("p (k d) -> p k d", k=2),
                                    a_hi[:, 4 * q + r:4 * q + r + 3:2, :].bitcast(F32),
                                    ALU.subtract).then_inc(a_rest, 1)
            dve.wait_ge(x1_in, 16)
            measure_x(xres[:, 1], 1)
            dve.wait_ge(small_in, 32)
            v.tensor_tensor(cent_sq[:], centT[:], centT[:], ALU.mult).then_inc(norm_squares, 1)
            split_x(1, 1, U_BANK)
            dve.wait_ge(norm_ready, 1)
            v.tensor_copy(cent_norm[:], R_BANK[:, 0:EXPERTS]).then_inc(norm_taken, 1)
            dve.wait_ge(consts_made, 2)

            def group(g, par, has_prev, has_next):
                for t in range(TPG):
                    s = TPG * g + t
                    if t == 3 and has_next:
                        add_residual(s - 3, g, 0, par)
                    elif t < 3 and has_prev:
                        add_residual(s - 3, g - 1, t + 1, 1 - par)
                    if t == 2 and has_next:
                        split_x(g + 2, par)
                    if t >= 2 or has_prev:
                        normalise(s - 2, t % 2)
                    if t == 1 and has_next:
                        dve.wait_ge(x_in, 16 * (g + 2))
                        measure_x(xin, g + 2)
                    if t == 2 and has_prev and has_next:
                        measure_x2(g - 1)
                    if t == 3 and has_prev and has_next:
                        add_norms(g - 1)
                        choose(g - 1)

                    def scale_rows():
                        scaled(g - 1, 1 - par)

                    def place_rows():
                        places(g - 1, 1 - par)

                    if t == 1 and not has_prev:
                        reduce_keys(None, s, 1)
                        reduce_keys(s - 1, None, 1)
                        continue
                    reduce_keys(s - 1 if t >= 1 or has_prev else None, s, t % 2,
                                {2: scale_rows, 3: place_rows}.get(t) if has_prev and has_next else None)
                    if t == 2 and not has_next:
                        measure_x2(g - 1)

            group(0, 0, False, True)
            with dve.Fori(0, LOOPS) as i:
                seq.loop(i, DVE_PER_TURN)
                for k in range(2):
                    group(1 + k + 2 * i, (1 + k) % 2, True, True)
                seq.end_loop(LOOPS)
            last = GROUPS - 1
            group(last, last % 2, True, False)
            normalise(TILES - 2, 0)
            add_residual(TILES - 4, last, 0, last % 2)
            add_residual(TILES - 3, last, 1, last % 2)
            scaled(last - 1, 1 - last % 2)
            split_up((0,))
            reduce_keys(TILES - 1, None, 0)
            add_norms(last - 1)
            choose(last - 1)
            normalise(TILES - 1, 1)
            places(last - 1, 1 - last % 2)
            add_residual(TILES - 2, last, 2, last % 2)
            dve.wait_ge(x2_done, TILES - 1)
            gather(x2, stats2, range(TPG - 1))
            split_up(range(1, UP_PIECES))
            add_residual(TILES - 1, last, 3, last % 2)
            measure_x2(last, TPG - 1)
            dve.wait_ge(root2_done, last + 1)
            for t in range(TPG):
                norm = v.tensor_scalar(xl[:, t, :], x2[:, t, :], mv2[:, t, 0:1], root2[:, 0, t:t + 1],
                                       ALU.subtract, ALU.mult)
            norm.then_inc(xl_done, 1)
            scaled(last, last % 2)
            add_norms(last)
            choose(last)
            places(last, last % 2)

            dve.wait_ge(counts_ready, 1)
            seq.then(v.tensor_copy(count[:], MISC[:, 0:EXPERTS]))
            seq.mark(v.tensor_tensor(pad_at[:], count[:], region_of[:], ALU.add))
            seq.then(v.tensor_scalar(count_i[:], count[:], float(P - 1), None, ALU.add))
            seq.mark(v.tensor_scalar(count_i[:], count_i[:], P.bit_length() - 1, None, ALU.logical_shift_right))
            seq.wait()
            v.tensor_copy(pad_i[:], pad_at[:]).then_inc(pads_found, 1)
            seq.then(v.tensor_copy(ntile[:], count_i[:]))
            seq.then(v.tensor_tensor(upto[:], upto[:], ntile[:].unsqueeze(1).to_broadcast([P, EXPERTS, EXPERTS]),
                                     ALU.mult))
            seq.then(v.tensor_reduce(cumul[:], upto[:], AX_X, ALU.add))
            seq.then(v.tensor_tensor(done[:], tile_no[:].unsqueeze(2).to_broadcast([P, FT, EXPERTS]),
                                     cumul[:].unsqueeze(1).to_broadcast([P, FT, EXPERTS]), ALU.is_ge))
            seq.mark(v.tensor_reduce(tile_e[:], done[:], AX_X, ALU.add))
            seq.then(v.tensor_tensor(done_n[:], done[:], ntile[:].unsqueeze(1).to_broadcast([P, FT, EXPERTS]),
                                     ALU.mult))
            seq.then(v.tensor_reduce(tile_b[:], done_n[:], AX_X, ALU.add))
            seq.then(v.tensor_tensor(tile_b[:], tile_no[:], tile_b[:], ALU.subtract))
            seq.mark(v.tensor_scalar(tile_r[:], tile_e[:], float(REGION), None, ALU.mult))
            seq.then(v.tensor_scalar(tile_e[:], tile_e[:], float(EXPERTS - 1), None, ALU.min))
            seq.then(v.scalar_tensor_tensor(out=tile_r[:], in0=tile_b[:], scalar=float(P), in1=tile_r[:],
                                            op0=ALU.mult, op1=ALU.add))
            pairs = tile_e[:].rearrange("p (j n) -> p j n", n=2)
            seq.mark(v.memset(pair_e[:], 0.0))
            seq.wait()
            seq.then(v.scalar_tensor_tensor(out=pair_e[:, 2:FT // 2 + 2], in0=pairs[:, :, 1], scalar=float(EXPERTS),
                                            in1=pairs[:, :, 0], op0=ALU.mult, op1=ALU.add))
            seq.then(v.scalar_tensor_tensor(out=four_e[:], in0=pair_e[:, 2:], scalar=float(EXPERTS ** 2),
                                            in1=pair_e[:, 0:FT // 2 + 2], op0=ALU.mult, op1=ALU.add))
            seq.mark(v.tensor_copy(t_experts[:], four_e[:]))
            seq.mark(v.tensor_scalar(tile_r[:], tile_r[:], float(EXPERTS * REGION), None, ALU.min))
            seq.wait()
            seq.then(v.tensor_copy(t_row[:], tile_r[:]))
            v.memset(spare_v[:], 0.0).then_inc(tiles_found, 1)

            def pair(j, k, turn, static):
                if static < FT:
                    dve.wait_ge(fxT_hi_out, FB // 2 * turn + k // 2 + 1)
                    v.tensor_tensor(fxT_lo[:], TURN_BANK[:, 0:2 * P], fxT_hi[:].bitcast(F32),
                                    ALU.subtract).then_inc(fxT_lo_out, 1)
                if static >= LAG:
                    b = (k - LAG) % FB
                    for n in range(2):
                        v.tensor_copy(numbers[:, b + n:b + n + 1],
                                      frow[:, b + n, ID_AT:ID_AT + 1]).then_inc(numbers_taken, 1)
                        dve.wait_ge(down_ready, j + n - LAG + 1)
                        v.tensor_tensor(fout[:, b + n, :], DOWN_BANK[n][:, 0:D], frow[:, b + n, D:2 * D],
                                        ALU.add).then_inc(fout_done, 1)
                if static < FT:
                    for n in range(2):
                        dve.wait_ge(gated, j + n + 1)
                        if static >= FB:
                            dve.wait_ge(stored[k + n], 16 * turn)
                        v.tensor_tensor(act[:, n, :], gate[:, n, :], UP_BANK[n][:, 0:HID],
                                        ALU.mult).then_inc(act_done, 1)

            ffn_pairs(dve, pair, drain=True)


DVE_PER_TURN = 220


def kernel(x, ctx_1024, L0_xattn_Wq, L0_xattn_Wk, L0_xattn_Wv, L0_xattn_Wo, L0_ffn_scale, L0_ffn_centroids,
           L0_ffn_up_w, L0_ffn_down_w):
    import numpy as np
    from concourse import bacc
    from concourse.bass_utils import run_bass_kernel_spmd

    def lay(a):
        return np.ascontiguousarray(a)

    flat = np.asarray(ctx_1024).reshape(TOKENS, D)
    arrays = {
        "x": lay(np.asarray(x).reshape(TOKENS, D)),
        "ctx": lay(flat),
        "ctx_t": lay(flat.T),
        "wq_t": lay(np.asarray(L0_xattn_Wq).T),
        "wk_t": lay(np.asarray(L0_xattn_Wk).T),
        "wv_t": lay(np.asarray(L0_xattn_Wv).T),
        "wo": lay(L0_xattn_Wo),
        "scale": lay(np.asarray(L0_ffn_scale).reshape(1, D)),
        "cent_t": lay(np.asarray(L0_ffn_centroids).T),
        "up_w": lay(L0_ffn_up_w),
        "down_w": lay(L0_ffn_down_w),
    }
    nc = bacc.Bacc("TRN2", target_bir_lowering=False, num_devices=1)
    args = [nc.dram_tensor(n, a.shape, mybir.dt.from_np(a.dtype), kind="ExternalInput").ap()
            for n, a in arrays.items()]
    out = nc.dram_tensor("out", (TOKENS, D), F32, kind="ExternalOutput").ap()
    xattn_ffn(nc, *args, out)
    r = run_bass_kernel_spmd(nc, [arrays], core_ids=[0])
    return r.results[0]["out"].reshape(TOKENS // SEQ, SEQ, D)
```
